# Optimizing a Trainium2 kernel written in Bass

```python
import numpy as np
import jax
import jax.numpy as jnp

def _softmax(x, axis=-1):
    return jax.nn.softmax(x, axis=axis)

def _gelu(x):
    return jax.nn.gelu(x, approximate=True)

def _silu(x):
    return jax.nn.silu(x)

def _sigmoid(x):
    return jax.nn.sigmoid(x)

def _layernorm(x, axis=-1, eps=1e-05):
    m = jnp.mean(x, axis=axis, keepdims=True)
    v = jnp.var(x, axis=axis, keepdims=True)
    return (x - m) / jnp.sqrt(v + eps)

def _scatter_add(tgt, idx, src, axis=0):
    return tgt.at[idx].add(src)

def _segment_sum(src, seg, n):
    return jax.ops.segment_sum(src, seg, n)
kernel_name = 'mk_decoder_postln_d1_seqx_r4_27f9b8'

def setup_inputs(seed: int=0):
    np.random.seed(seed)
    _w = jnp.asarray

    def _rec_inputs():
        import jax
        import jax.numpy as jnp
        _rk = jax.random.key(seed)
        x = -0.0002928 + 1 * jax.random.normal(jax.random.fold_in(_rk, 1), (2, 1024, 256), jnp.float32)
        _lenS = 1024 - jax.random.randint(jax.random.fold_in(_rk, 7), (2,), 0, max(1, 1024 // 4) + 1, jnp.int32)
        _lenS2 = 77 - jax.random.randint(jax.random.fold_in(_rk, 8), (2,), 0, max(1, 77 // 4) + 1, jnp.int32)
        _ctx_1024P = jax.random.normal(jax.random.fold_in(_rk, 11), (2, 16, 256), jnp.float32)
        _ctx_1024c = jax.random.dirichlet(jax.random.fold_in(_rk, 511), 0.3 * jnp.ones((16,), jnp.float32), (2, 77))
        _ctx_1024t = jnp.einsum('bsk,bkd->bsd', _ctx_1024c, _ctx_1024P)
        _ctx_1024t = _ctx_1024t * jax.lax.rsqrt(jnp.mean(jnp.square(_ctx_1024t)) + 1e-12) * 0.953939
        ctx_1024 = 4.13588e-05 + 0.999923 * (_ctx_1024t + 0.3 * jax.random.normal(jax.random.fold_in(_rk, 611), (2, 77, 256), jnp.float32))
        return (x, ctx_1024)
    x, ctx_1024 = _rec_inputs()

    def _L0_attn_setup():
        import jax, jax.numpy as jnp
        import numpy as np
        HEADS = 16
        DIM_HEAD = 64
        B, T, C = (4, 512, 256)

        def apply_rope(x):
            d = x.shape[-1]
            seq_len = x.shape[1]
            inv_freq = 1.0 / 10000.0 ** (jnp.arange(0, d, 2, dtype=jnp.float32) / d)
            pos = jnp.arange(seq_len, dtype=jnp.float32)
            ang = pos[:, None] * inv_freq[None, :]
            sin = jnp.sin(ang)[None]
            cos = jnp.cos(ang)[None]
            x1, x2 = (x[..., 0::2], x[..., 1::2])
            rot = jnp.stack([x1 * cos - x2 * sin, x1 * sin + x2 * cos], axis=-1)
            return rot.reshape(x.shape)
        key = jax.random.key(seed)
        ks = jax.random.split(key, 6)
        inner = HEADS * DIM_HEAD
        w = 0.02
        return {'x': jax.random.normal(ks[0], (B, T, C), dtype=jnp.float32), 'Wq': jax.random.normal(ks[1], (C, inner), dtype=jnp.float32) * w, 'Wk': jax.random.normal(ks[2], (C, inner), dtype=jnp.float32) * w, 'Wv': jax.random.normal(ks[3], (C, inner), dtype=jnp.float32) * w, 'Wo': jax.random.normal(ks[4], (inner, C), dtype=jnp.float32) * w, 'bo': jnp.zeros((C,), dtype=jnp.float32)}
    _L0_attn_all = _L0_attn_setup()
    _L0_attn_in = {k: v for k, v in _L0_attn_all.items() if k in ('Wq', 'Wk', 'Wv', 'Wo', 'bo')}
    del _L0_attn_all

    def _L0_xattn_setup():
        import jax, jax.numpy as jnp
        import numpy as np
        HIDDEN = 256
        HEADS = 16
        HEAD_DIM = 64
        key = jax.random.key(seed)
        ks = jax.random.split(key, 7)
        B, Q, K = (2, 512, 1024)
        s = 1.0 / np.sqrt(HIDDEN)
        return {'query': jax.random.normal(ks[0], (B, Q, HIDDEN), dtype=jnp.float32), 'key': jax.random.normal(ks[1], (B, K, HIDDEN), dtype=jnp.float32), 'value': jax.random.normal(ks[2], (B, K, HIDDEN), dtype=jnp.float32), 'w_q': jax.random.normal(ks[3], (HIDDEN, HEADS * HEAD_DIM), dtype=jnp.float32) * s, 'w_k': jax.random.normal(ks[4], (HIDDEN, HEADS * HEAD_DIM), dtype=jnp.float32) * s, 'w_v': jax.random.normal(ks[5], (HIDDEN, HEADS * HEAD_DIM), dtype=jnp.float32) * s, 'w_o': jax.random.normal(ks[6], (HEADS * HEAD_DIM, HIDDEN), dtype=jnp.float32) * s}
    _L0_xattn_all = _L0_xattn_setup()
    _L0_xattn_in = {k: v for k, v in _L0_xattn_all.items() if k in ('w_q', 'w_k', 'w_v', 'w_o')}
    del _L0_xattn_all

    def _L0_ffn_setup():
        import jax, jax.numpy as jnp
        import numpy as np
        CAPACITY = 0.5
        key = jax.random.key(seed)
        ks = jax.random.split(key, 7)
        b, s, d, h = (4, 2048, 256, 1024)
        sc_r = 1.0 / np.sqrt(d)
        sc_1 = 1.0 / np.sqrt(d)
        sc_2 = 1.0 / np.sqrt(h)
        return {'x': jax.random.normal(ks[0], (b, s, d), dtype=jnp.float32), 'w_r': jax.random.uniform(ks[1], (d, 1), jnp.float32, -sc_r, sc_r), 'b_r': jax.random.uniform(ks[2], (1,), jnp.float32, -sc_r, sc_r), 'W1': jax.random.uniform(ks[3], (d, h), jnp.float32, -sc_1, sc_1), 'b1': jax.random.uniform(ks[4], (h,), jnp.float32, -sc_1, sc_1), 'W2': jax.random.uniform(ks[5], (h, d), jnp.float32, -sc_2, sc_2), 'b2': jax.random.uniform(ks[6], (d,), jnp.float32, -sc_2, sc_2)}
    _L0_ffn_all = _L0_ffn_setup()
    _L0_ffn_in = {k: v for k, v in _L0_ffn_all.items() if k in ('w_r', 'b_r', 'W1', 'b1', 'W2', 'b2')}
    del _L0_ffn_all
    return {'x': x, 'ctx_1024': ctx_1024, 'L0_attn_Wq': _L0_attn_in['Wq'], 'L0_attn_Wk': _L0_attn_in['Wk'], 'L0_attn_Wv': _L0_attn_in['Wv'], 'L0_attn_Wo': _L0_attn_in['Wo'], 'L0_attn_bo': _L0_attn_in['bo'], 'L0_xattn_w_q': _L0_xattn_in['w_q'], 'L0_xattn_w_k': _L0_xattn_in['w_k'], 'L0_xattn_w_v': _L0_xattn_in['w_v'], 'L0_xattn_w_o': _L0_xattn_in['w_o'], 'L0_ffn_w_r': _L0_ffn_in['w_r'], 'L0_ffn_b_r': _L0_ffn_in['b_r'], 'L0_ffn_W1': _L0_ffn_in['W1'], 'L0_ffn_b1': _L0_ffn_in['b1'], 'L0_ffn_W2': _L0_ffn_in['W2'], 'L0_ffn_b2': _L0_ffn_in['b2']}

def reference(x, ctx_1024, L0_attn_Wq, L0_attn_Wk, L0_attn_Wv, L0_attn_Wo, L0_attn_bo, L0_xattn_w_q, L0_xattn_w_k, L0_xattn_w_v, L0_xattn_w_o, L0_ffn_w_r, L0_ffn_b_r, L0_ffn_W1, L0_ffn_b1, L0_ffn_W2, L0_ffn_b2):
    import jax
    import jax.numpy as jnp

    def _L0_attn_ref(x, Wq, Wk, Wv, Wo, bo):
        import jax, jax.numpy as jnp
        import numpy as np
        HEADS = 16
        DIM_HEAD = 64
        B, T, C = (4, 512, 256)

        def apply_rope(x):
            d = x.shape[-1]
            seq_len = x.shape[1]
            inv_freq = 1.0 / 10000.0 ** (jnp.arange(0, d, 2, dtype=jnp.float32) / d)
            pos = jnp.arange(seq_len, dtype=jnp.float32)
            ang = pos[:, None] * inv_freq[None, :]
            sin = jnp.sin(ang)[None]
            cos = jnp.cos(ang)[None]
            x1, x2 = (x[..., 0::2], x[..., 1::2])
            rot = jnp.stack([x1 * cos - x2 * sin, x1 * sin + x2 * cos], axis=-1)
            return rot.reshape(x.shape)
        b, t, c = x.shape
        h, d = (HEADS, DIM_HEAD)
        scale = d ** (-0.5)

        def split_heads(z):
            return z.reshape(b, t, h, d).transpose(0, 2, 1, 3).reshape(b * h, t, d)
        q = split_heads(x @ Wq)
        k = split_heads(x @ Wk)
        v = split_heads(x @ Wv)
        q = apply_rope(q)
        k = apply_rope(k)
        sim = jnp.einsum('bid,bjd->bij', q, k) * scale
        causal = jnp.tril(jnp.ones((t, t), dtype=bool))
        sim = jnp.where(causal[None], sim, -jnp.inf)
        attn = jax.nn.softmax(sim, axis=-1)
        out = jnp.einsum('bij,bjd->bid', attn, v)
        out = out.reshape(b, h, t, d).transpose(0, 2, 1, 3).reshape(b, t, h * d)
        return out @ Wo + bo

    def _L0_xattn_ref(query, key, value, w_q, w_k, w_v, w_o):
        import jax, jax.numpy as jnp
        import numpy as np
        HIDDEN = 256
        HEADS = 16
        HEAD_DIM = 64
        B, Q, _ = query.shape
        Kl = key.shape[1]
        scale = HEAD_DIM ** (-0.5)
        q = (query @ w_q).reshape(B, Q, HEADS, HEAD_DIM).transpose(0, 2, 1, 3)
        k = (key @ w_k).reshape(B, Kl, HEADS, HEAD_DIM).transpose(0, 2, 1, 3)
        v = (value @ w_v).reshape(B, Kl, HEADS, HEAD_DIM).transpose(0, 2, 1, 3)
        scores = jnp.einsum('bhqd,bhkd->bhqk', q, k) * scale
        attn = jax.nn.softmax(scores, axis=-1)
        out = jnp.einsum('bhqk,bhkd->bhqd', attn, v)
        out = out.transpose(0, 2, 1, 3).reshape(B, Q, HEADS * HEAD_DIM)
        return out @ w_o

    def _L0_ffn_ref(x, w_r, b_r, W1, b1, W2, b2):
        import jax, jax.numpy as jnp
        import numpy as np
        CAPACITY = 0.5
        b, s, d = x.shape
        k = int(CAPACITY * s)
        weights = (jnp.einsum('bsd,do->bso', x, w_r) + b_r).squeeze(-1)
        top_vals, _ = jax.lax.top_k(weights, k)
        threshold = top_vals[:, -1]
        selected = weights > threshold[:, None]
        hidden = jax.nn.gelu(jnp.einsum('bsd,dh->bsh', x, W1) + b1, approximate=False)
        blk = jnp.einsum('bsh,hd->bsd', hidden, W2) + b2
        m = selected[..., None]
        return jnp.where(m, blk, x)
    x = _layernorm(x + _L0_attn_ref(x, L0_attn_Wq, L0_attn_Wk, L0_attn_Wv, L0_attn_Wo, L0_attn_bo), axis=-1)
    x = _layernorm(x + _L0_xattn_ref(x, ctx_1024, ctx_1024, L0_xattn_w_q, L0_xattn_w_k, L0_xattn_w_v, L0_xattn_w_o), axis=-1)
    x = _layernorm(x + _L0_ffn_ref(x, L0_ffn_w_r, L0_ffn_b_r, L0_ffn_W1, L0_ffn_b1, L0_ffn_W2, L0_ffn_b2), axis=-1)
    return x

_drawn_inputs = setup_inputs


def setup_inputs(seed=0):
    import zlib

    import numpy as np

    out = dict(_drawn_inputs(seed))
    spreads = {'L0_attn_bo': (0.0, 0.1)}
    factors = {'L0_attn_Wq': 8.0,
     'L0_attn_Wk': 8.0,
     'L0_attn_Wv': 3.347,
     'L0_attn_Wo': 3.65,
     'L0_ffn_b1': 6.862,
     'L0_ffn_b2': 4.42}
    for name, (base, spread) in spreads.items():
        noise = np.random.default_rng([zlib.crc32(name.encode()), seed]).standard_normal(out[name].shape)
        drawn = base * np.exp(spread * noise) if base else spread * noise
        out[name] = jnp.asarray(drawn.astype(out[name].dtype))
    for name, factor in factors.items():
        out[name] = (out[name] * factor).astype(out[name].dtype)
    return out
```

```python
import concourse.bass as bass
from concourse import mybir
from contextlib import ExitStack

F = mybir.dt.float32
R = mybir.dt.float32r
BF = mybir.dt.bfloat16
ALU = mybir.AluOpType
ACT = mybir.ActivationFunctionType
AX = mybir.AxisListType

NB, T, C, NH, D = 2, 1024, 256, 16, 64
L = 77
LP = 78
NP = NH // 2
NT = T // 128
TOP = 512
NEG = -1.0e30
EPS = 1e-5
SWAP = [i ^ 1 for i in range(32)]


class Engine:

    def __init__(self, sem):
        self.sem, self.count, self.queue, self.seen = sem, 0, [], {}

    def wait(self, *tokens):
        for tok in tokens:
            if tok is None:
                continue
            if isinstance(tok, list):
                self.wait(*tok)
                continue
            sem, value = tok
            if self.seen.get(sem, 0) < value:
                self.seen[sem] = value
                self.queue.append(lambda e, s=sem, v=value: e.wait_ge(s, v))

    def do(self, fn, *waits):
        self.wait(*waits)
        self.count += 1
        self.queue.append(lambda e: fn(e).then_inc(self.sem, 1))
        return (self.sem, self.count)

    def run(self, e):
        for f in self.queue:
            f(e)


def build(nc, xT, x, cT, Wq, Wk, Wv, Wo, bo, cq, ck, cv, co, wr, br, W1, b1, W2, b2, cosT, sinT,
          identd, maskqk, maskkq, out):
    ctx = ExitStack()
    with ctx:
        def sb(name, shape, dt=F):
            return ctx.enter_context(nc.sbuf_tensor(name, shape, dt))

        def sem(name):
            return ctx.enter_context(nc.semaphore(name))

        PE, AC, DV, PO, SP = (Engine(sem(n)) for n in ("s_pe", "s_act", "s_dve", "s_pool", "s_sp"))
        dma_sems = {}

        def load(name, dst, src, *waits):
            SP.wait(*waits)
            if name not in dma_sems:
                dma_sems[name] = [sem("d_" + name), 0]
            d = dma_sems[name]
            d[1] += 16
            SP.queue.append(lambda e: e.dma_start(dst, src).then_inc(d[0], 16))
            return (d[0], d[1])

        Wraw = [sb(f"Wraw{i}", [128, 2048]) for i in range(4)]
        SLH = [sb(f"SLH{i}", [128, 512], R) for i in range(3)]
        SLL = [sb(f"SLL{i}", [128, 512], R) for i in range(3)]
        REG = sb("REG", [128, 16384], R)
        XH = sb("XH", [128, 2, T], R)
        XL = sb("XL", [128, 2, T], R)
        VV = [sb(f"VV{i}", [128, NT, 384]) for i in range(2)]
        OH = sb("OH", [128, T], R)
        OL = sb("OL", [128, T], R)
        OF = sb("OF", [128, T])
        X = sb("X", [128, NB, NT, C])
        PT = [sb(f"PT{i}", [128, 512]) for i in range(3)]
        cosS = sb("cosS", [128, T])
        sinS = sb("sinS", [128, T])
        T1 = [sb(f"T1{i}", [128, 512]) for i in range(2)]
        SH = [sb(f"SH{i}", [128, 512]) for i in range(2)]
        RC = sb("RC", [128, 512])
        CH = sb("CH", [128, NB, 2, LP], R)
        CL = sb("CL", [128, NB, 2, LP], R)
        NM = [sb(f"NM{i}", [128, 12]) for i in range(2)]
        MR = [sb(f"MR{i}", [128, NT, 2], R) for i in range(2)]
        idF = sb("idF", [128, 128])
        idR = sb("idR", [128, 128], R)
        idB = sb("idB", [128, 128], BF)
        mQK = sb("mQK", [128, 128], BF)
        mKQ = sb("mKQ", [128, 128], BF)
        boS = sb("boS", [128, C])
        wrS = sb("wrS", [128, C])
        b1S = sb("b1S", [128, NT])
        brS = sb("brS", [128, 1])
        st = sb("st", [128, NT, 6])
        mv = sb("mv", [128, NT, 2])
        rs = sb("rs", [128, NT])
        half = sb("half", [128, NT])
        wl = sb("wl", [128, NT])
        cnt = sb("cnt", [128, NT, 2])
        sel = sb("sel", [128, NT])

        bank = [ctx.enter_context(nc.psum_tensor(f"bank{i}", [128, 512], F)) for i in range(8)]
        ST, OB, RB = bank[0:2], bank[2:4], bank[4:8]
        block = ctx.enter_context(nc.Block())

        def setview(kind, par, buf):
            o = ((par * 2 + buf) * 4 + kind) * 1024
            return REG[:, o:o + 1024]

        ring = [0, [None] * 4]

        def take():
            i = ring[0] % 4
            ring[0] += 1
            return RB[i], ring[1][i], i

        def free(i, tok):
            ring[1][i] = tok

        raw_free = [None] * 4
        raw_tok = {}

        def load_w(key, slot, ap):
            raw_tok[key] = load(key, Wraw[slot][:, :], ap, raw_free[slot])

        stage = {"free": [None] * 2, "n": 0}
        tmp_free = [None] * 2

        ld_cst = load("cst", idF[:, :], identd)
        mtmp = load("msk", T1[0][:, 0:128], maskqk)
        mtmp = load("msk", T1[0][:, 128:256], maskkq)
        load_w("wv0", 2, Wv)
        xT_ready = {}

        k_idr = AC.do(lambda e: e.activation(idR[:, :], idF[:, :], ACT.Copy), ld_cst)
        k_idb = AC.do(lambda e: e.activation(idB[:, :], idF[:, :], ACT.Copy), ld_cst)
        k_mqk = AC.do(lambda e: e.activation(mQK[:, :], T1[0][:, 0:128], ACT.Copy), mtmp)
        k_mkq = AC.do(lambda e: e.activation(mKQ[:, :], T1[0][:, 128:256], ACT.Copy), mtmp)
        k_cst = [k_idr, k_idb, k_mqk, k_mkq]
        tmp_free[0] = k_mkq

        xh_free = [None]
        xh_tok = [None]
        tn = [0]

        def load_xT(b):
            toks = []
            for j in range(4):
                i = tn[0] % 2
                tn[0] += 1
                kt, c = j // 2, j % 2
                t = load(f"xT{i}", T1[i][:, :], xT[b, kt * 128:kt * 128 + 128, c * 512:c * 512 + 512],
                         tmp_free[i])
                h = XH[:, kt, c * 512:c * 512 + 512]
                l = XL[:, kt, c * 512:c * 512 + 512]
                a = AC.do(lambda e, h=h, i=i: e.activation(h, T1[i][:, :], ACT.Copy), t, xh_free[0])
                d = DV.do(lambda e, h=h, l=l, i=i: e.tensor_tensor(l, T1[i][:, :], h.bitcast(F), ALU.subtract),
                          a, t, xh_free[0])
                tmp_free[i] = d
                toks += [a, d]
            xh_tok[0] = toks

        load_xT(0)
        load_w("wq0", 0, Wq)
        load_w("wk0", 1, Wk)
        ld_rope = load("rope", cosS[:, :], cosT)
        ld_rope = load("rope", sinS[:, :], sinT)
        load_w("wo0", 3, Wo)
        ld_x = [load(f"x{b}", X[:, b, :, :], x[b].rearrange("(n p) c -> p n c", p=128)) for b in range(NB)]
        ld_bo = load("bo", boS[:, :], bo)
        ld_sm = load("sm", wrS[:, :], wr)
        ld_sm = load("sm", b1S[:, :], b1)
        ld_sm = load("sm", brS[:, :], br)

        k_ones = [PO.do(lambda e, v=v: e.memset(
            v[:, :, :].rearrange("p t (a s d) -> p t a s d", a=2, s=3)[:, :, :, 1, :], 1.0)) for v in VV]
        k_half = PO.do(lambda e: e.memset(half[:, :], -0.5))
        k_aug = {}
        z = k_half
        for par in range(2):
            for buf in range(2):
                aug = 64 * (1 - par)
                q2, k2 = setview(1, par, buf), setview(3, par, buf)
                z = PO.do(lambda e, a=q2[aug:aug + 64, :].bitcast(F): e.memset(a, 0.0), z)
                z = PO.do(lambda e, a=k2[aug:aug + 64, :].bitcast(F): e.memset(a, 0.0), z)
                z = PO.do(lambda e, a=k2[aug:aug + 2, :].bitcast(F): e.memset(a, 1.0), z)
                k_aug[par, buf] = z
        PO.wait(z)

        sl = {"n": 0, "free": [None] * 3}

        def split(parts, key):
            i = sl["n"] % 3
            sl["n"] += 1
            o, toks = 0, []
            for raw, slot, tok in parts:
                shp = raw.shape[1:]
                n = 1
                for s in shp:
                    n *= s
                h, l = SLH[i][:, o:o + n], SLL[i][:, o:o + n]
                if len(shp) == 2:
                    h = h.rearrange("p (a b) -> p a b", a=shp[0])
                    l = l.rearrange("p (a b) -> p a b", a=shp[0])
                a = PO.do(lambda e, h=h, r=raw: e.tensor_copy(h, r), tok, sl["free"][i])
                d = PO.do(lambda e, h=h, l=l, r=raw: e.tensor_tensor(l, r, h.bitcast(F), ALU.subtract),
                          a, sl["free"][i])
                raw_free[slot] = d
                toks.append(d)
                o += n
            return i, toks[-1]

        def wview(slot):
            return Wraw[slot][:, :].rearrange("p (k n) -> p k n", k=2)

        def woview(slot):
            return Wraw[slot][:, :].rearrange("p (k n) -> p k n", k=8)

        def mm3(e, o, terms):
            for n, (a, b) in enumerate(terms):
                last = e.matmul(o, a, b, start=n == 0, stop=n == len(terms) - 1)
            return last

        set_free = {}
        set_tok = {}
        P_free = [None] * 3

        def prep(u, pair):
            kind, b = u
            buf = (uidx[u] * NP + pair) % 2
            key = "0" if kind == "self" else "1"
            pc = slice(pair * 128, pair * 128 + 128)
            pieces = []
            box = {}

            def start():
                box["s"], box["t"] = split([(wview(0)[:, :, pc], 0, raw_tok["wq" + key]),
                                            (wview(1)[:, :, pc], 1, raw_tok["wk" + key])], key)
                for par in range(2):
                    set_tok[u, pair, par] = [k_aug[par, buf]]

            def proj(which, c):
                s = box["s"]
                wh = SLH[s][:, which * 256:which * 256 + 256].rearrange("p (k n) -> p k n", k=2)
                wlo = SLL[s][:, which * 256:which * 256 + 256].rearrange("p (k n) -> p k n", k=2)
                if kind == "self" or which == 0:
                    w = 512
                    xh = [XH[:, k, c * 512:c * 512 + 512] for k in range(2)]
                    xl = [XL[:, k, c * 512:c * 512 + 512] for k in range(2)]
                    dep = xh_tok[0]
                else:
                    w = LP
                    xh = [CH[:, b, k, :] for k in range(2)]
                    xl = [CL[:, b, k, :] for k in range(2)]
                    dep = ctx_tok[0]
                bk, ready, i = take()
                terms = []
                for k in range(2):
                    terms += [(wh[:, k, :], xh[k]), (wh[:, k, :], xl[k]), (wlo[:, k, :], xh[k])]
                p = PE.do(lambda e: mm3(e, bk[:, 0:w], terms), box["t"], dep, ready)
                sl["free"][s] = p
                if kind == "self" or which == 0:
                    xh_free[0] = p
                cs = slice(c * 512, c * 512 + w)
                if kind == "self":
                    j = tn[0] % 2
                    tn[0] += 1
                    a = DV.do(lambda e: e.tensor_tensor(T1[j][:, :], bk[:, :], cosS[:, cs], ALU.mult),
                              p, ld_rope, tmp_free[j])
                    d = DV.do(lambda e: e.stream_shuffle(SH[j][:, :], bk[:, :], SWAP))
                    free(i, d)
                    g = PO.do(lambda e: e.tensor_tensor(SH[j][:, :], SH[j][:, :], sinS[:, cs], ALU.mult),
                              d, ld_rope)
                    g = PO.do(lambda e: e.tensor_tensor(T1[j][:, :], T1[j][:, :], SH[j][:, :], ALU.add),
                              g, a)
                    src, dep2 = T1[j][:, :], g
                else:
                    src, dep2 = bk[:, 0:w], p
                hi = []
                for par in range(2):
                    base = 64 * par
                    t = setview(0 if which == 0 else 2, par, buf)[base:base + 64, cs]
                    hi.append(AC.do(lambda e, t=t, s=src[base:base + 64, :]: e.activation(t, s, ACT.Copy),
                                    dep2, set_free.get((par, buf))))
                lo = []
                for par in range(2):
                    base, aug = 64 * par, 64 * (1 - par)
                    t = setview(0 if which == 0 else 2, par, buf)[base:base + 64, cs]
                    l = (setview(0, par, buf)[aug:aug + 64, cs] if which == 0
                         else setview(3, par, buf)[base:base + 64, cs])
                    lo.append(DV.do(lambda e, t=t, l=l, s=src[base:base + 64, :]: e.tensor_tensor(
                        l, s, t.bitcast(F), ALU.subtract), hi, dep2, set_free.get((par, buf))))
                if kind == "self":
                    tmp_free[j] = lo[-1]
                else:
                    free(i, lo[-1])
                for par in range(2):
                    base, aug = 64 * par, 64 * (1 - par)
                    t = setview(0 if which == 0 else 2, par, buf)[base:base + 64, cs]
                    dup = (setview(1, par, buf)[base:base + 64, cs] if which == 0
                           else setview(2, par, buf)[aug:aug + 64, cs])
                    k = AC.do(lambda e, t=t, dup=dup: e.activation(dup, t.bitcast(F), ACT.Copy),
                              hi[par], set_free.get((par, buf)))
                    set_tok[u, pair, par] += [k, lo[par]]

            order = [(1, 0), (0, 0), (1, 1), (0, 1)] if kind == "self" else [(1, 0), (0, 0), (0, 1)]
            for n, (w_, c_) in enumerate(order):
                def piece(n=n, w_=w_, c_=c_):
                    if n == 0:
                        start()
                    proj(w_, c_)
                pieces.append(piece)
            return pieces

        vv_free = [None] * 2
        vv_tok = {}

        def vgroup(u, g):
            kind, b = u
            v = (uidx[u] * 4 + g) % 2
            key = "0" if kind == "self" else "1"
            box = {}

            def start():
                box["s"], box["t"] = split([(wview(2)[:, :, g * 256:g * 256 + 256], 2, raw_tok["wv" + key])], key)
                vv_tok[u, g] = [k_ones[v]]

            def piece(j):
                s = box["s"]
                wh = SLH[s][:, :].rearrange("p (k n) -> p k n", k=2)
                wlo = SLL[s][:, :].rearrange("p (k n) -> p k n", k=2)
                bk, ready, i = take()
                tiles = [2 * j, 2 * j + 1] if kind == "self" else [0]
                rows = 128 if kind == "self" else L

                def mms(e):
                    for n, t in enumerate(tiles):
                        if kind == "self":
                            xh = [XH[:, k, t * 128:t * 128 + 128] for k in range(2)]
                            xl = [XL[:, k, t * 128:t * 128 + 128] for k in range(2)]
                        else:
                            xh = [CH[:, b, k, 0:L] for k in range(2)]
                            xl = [CL[:, b, k, 0:L] for k in range(2)]
                        terms = []
                        for k in range(2):
                            terms += [(xh[k], wh[:, k, :]), (xh[k], wlo[:, k, :]), (xl[k], wh[:, k, :])]
                        last = mm3(e, bk[0:rows, n * 256:n * 256 + 256], terms)
                    return last
                p = PE.do(mms, box["t"], xh_tok[0] if kind == "self" else ctx_tok[0], ready)
                sl["free"][s] = p
                if kind == "self":
                    xh_free[0] = p
                for n, t in enumerate(tiles):
                    dst = VV[v][0:rows, t, :].rearrange("p (a s d) -> p a s d", a=2, s=3)[:, :, 0:3:2, :]
                    src = bk[0:rows, n * 256:n * 256 + 256].rearrange("p (a s d) -> p a s d", a=2, s=2)
                    k = AC.do(lambda e, dst=dst, src=src: e.activation(dst, src, ACT.Copy), p, vv_free[v])
                free(i, k)
                vv_tok[u, g].append(k)

            n = 4 if kind == "self" else 1

            def mk(j):
                def f():
                    if j == 0:
                        start()
                    piece(j)
                return f
            return [mk(j) for j in range(n)]

        nm_free = [None] * 2
        mr_free = [None] * 2

        def maxima(u, h):
            kind, b = u
            pair, par = h // 2, h % 2
            buf = (uidx[u] * NP + pair) % 2
            q1, k1 = setview(0, par, buf), setview(2, par, buf)
            m = h % 2
            toks = []
            pieces = []

            def chunk(qt, kc):
                k0 = kc * 512
                w = min(512, (qt + 1) * 128 - k0)
                diag = (qt + 1) * 128 <= k0 + 512
                col = qt if kc == 0 else 4 + qt
                bk, ready, i = take()

                def mms(e):
                    last = e.matmul(bk[:, 0:w], q1[:, qt * 128:qt * 128 + 128], k1[:, k0:k0 + w],
                                    start=True, stop=not diag)
                    if diag:
                        last = e.matmul(bk[:, w - 128:w], idB[:, :], mQK[:, :], start=False, stop=True)
                    return last
                p = PE.do(mms, set_tok[u, pair, par], k_cst, ready)
                d = DV.do(lambda e: e.tensor_reduce(NM[m][:, col:col + 1], bk[:, 0:w], AX.X, ALU.max,
                                                    negate=True), p, nm_free[m])
                free(i, d)
                toks.append(d)

            def chunk_x(j):
                bk, ready, i = take()

                def mms(e):
                    for n in range(4):
                        qt = 4 * j + n
                        last = e.matmul(bk[:, n * 128:n * 128 + LP], q1[:, qt * 128:qt * 128 + 128],
                                        k1[:, 0:LP], start=True, stop=True)
                    return last
                p = PE.do(mms, set_tok[u, pair, par], ready)
                d = DV.do(lambda e: e.tensor_reduce(
                    NM[m][:, 4 * j:4 * j + 4], bk[:, :].rearrange("p (n k) -> p n k", n=4)[:, :, 0:L],
                    AX.X, ALU.max, negate=True), p, nm_free[m])
                free(i, d)
                toks.append(d)

            if kind == "self":
                for qt in range(NT):
                    for kc in range(qt // 4 + 1):
                        pieces.append(lambda qt=qt, kc=kc: chunk(qt, kc))
            else:
                pieces = [lambda: chunk_x(0), lambda: chunk_x(1)]

            def combine():
                t = toks[-1]
                if kind == "self":
                    t = DV.do(lambda e: e.tensor_tensor(NM[m][:, 4:8], NM[m][:, 4:8], NM[m][:, 8:12], ALU.min), t)
                a = DV.do(lambda e: e.tensor_copy(MR[m][:, :, 0], NM[m][:, 0:8]), t, mr_free[m])
                d = DV.do(lambda e: e.tensor_tensor(MR[m][:, :, 1], NM[m][:, 0:8],
                                                    MR[m][:, :, 0].bitcast(F), ALU.subtract), a)
                nm_free[m] = d
                return d

            def rows():
                q2 = setview(1, par, buf)
                aug = 64 * (1 - par)
                d = mrd[0]

                def half_rows(c):
                    bk, ready, i = take()

                    def mms(e):
                        for n in range(4):
                            last = e.matmul(bk[0:2, n * 128:n * 128 + 128], MR[m][:, 4 * c + n, :],
                                            idR[:, :], start=True, stop=True)
                        return last
                    p = PE.do(mms, d, k_cst, ready)
                    k = AC.do(lambda e: e.activation(q2[aug:aug + 2, c * 512:c * 512 + 512], bk[0:2, :],
                                                     ACT.Copy), p, set_free.get((par, buf)))
                    free(i, k)
                    set_tok[u, pair, par].append(k)
                    mr_free[m] = p
                half_rows(0)
                half_rows(1)

            mrd = [None]

            def comb():
                mrd[0] = combine()
            pieces[-1] = (lambda f: (lambda: (f(), comb())))(pieces[-1])
            return pieces, rows

        st_free = [None] * 2
        o_free = [None] * 2
        of_free = [None]
        rc_free = [None]
        of_tok = {}
        sn, pn = [0], [0]
        x_tok = {}
        p_zero = []

        def attend(u, h, fill):
            kind, b = u
            pair, par = h // 2, h % 2
            buf = (uidx[u] * NP + pair) % 2
            q1, q2, k1, k2 = (setview(n, par, buf) for n in range(4))
            g, v = pair // 2, (uidx[u] * 4 + pair // 2) % 2
            vc = (pair % 2) * 192 + 64 * par
            base, den = 64 * par, 64 * (1 - par)
            rows = 128 if kind == "self" else L
            late = []

            def pv(c, kt, q0, w, i, ex):
                n = kt == 0
                last_kt = kt == (4 * c + 3 if kind == "self" else 0)
                o0 = q0 - c * 512
                p = PE.do(lambda e: e.matmul(OB[c][:, o0:o0 + w], VV[v][:, kt, vc:vc + 128], PT[i][:, 0:w],
                                             start=n, stop=last_kt),
                          ex, vv_tok[u, g], o_free[c] if n else None)
                P_free[i] = p
                if last_kt:
                    vv_free[v] = p
                    d = DV.do(lambda e: e.reciprocal(RC[base:base + 64, :], OB[c][den:den + 64, :]), p, rc_free[0])
                    d = DV.do(lambda e: e.tensor_tensor(OF[base:base + 64, c * 512:c * 512 + 512],
                                                        OB[c][base:base + 64, :], RC[base:base + 64, :],
                                                        ALU.mult), d, of_free[0])
                    rc_free[0] = d
                    o_free[c] = d
                    of_tok.setdefault((u, pair), []).append(d)

            n = 0
            for c in range(2):
                for kt in range(4 * (c + 1) if kind == "self" else 1):
                    q0 = max(kt * 128, c * 512) if kind == "self" else c * 512
                    w = (c + 1) * 512 - q0
                    s, i = sn[0] % 2, pn[0] % 3
                    sn[0] += 1
                    pn[0] += 1
                    diag = kind == "self" and kt * 128 >= c * 512
                    ks = slice(kt * 128, kt * 128 + rows)

                    def mms(e, s=s, q0=q0, w=w, ks=ks, diag=diag):
                        e.matmul(ST[s][0:rows, 0:w], k1[:, ks], q1[:, q0:q0 + w], start=True, stop=False)
                        last = e.matmul(ST[s][0:rows, 0:w], k2[:, ks], q2[:, q0:q0 + w],
                                        start=False, stop=not diag)
                        if diag:
                            last = e.matmul(ST[s][:, 0:128], idB[:, :], mKQ[:, :], start=False, stop=True)
                        return last
                    p = PE.do(mms, set_tok[u, pair, par], st_free[s])
                    ex = AC.do(lambda e, s=s, i=i, w=w: e.activation(
                        PT[i][0:rows, 0:w], ST[s][0:rows, 0:w], ACT.Exp, scale=D ** -0.5), p, P_free[i],
                        p_zero if kind == "cross" else None)
                    st_free[s] = ex
                    last_s = p
                    late.append((c, kt, q0, w, i, ex))
                    if len(late) > 1:
                        pv(*late.pop(0))
                    fill(n)
                    n += 1
            set_free[par, buf] = last_s
            while late:
                pv(*late.pop(0))

        oh_free = [None]

        def outproj(u, pair):
            kind, b = u
            key = "0" if kind == "self" else "1"
            box = {}

            def start():
                box["s"], box["t"] = split([(woview(3)[:, pair, :], 3, raw_tok["wo" + key])], key)
                a = AC.do(lambda e: e.activation(OH[:, :], OF[:, :], ACT.Copy), of_tok[u, pair], oh_free[0])
                d = PO.do(lambda e: e.tensor_tensor(OL[:, :], OF[:, :], OH[:, :].bitcast(F), ALU.subtract),
                          a, of_tok[u, pair], oh_free[0])
                of_free[0] = d
                box["o"] = [a, d]

            def piece(j):
                s = box["s"]
                bk, ready, i = take()
                wh, wlo = SLH[s][:, 0:256], SLL[s][:, 0:256]

                def mms(e):
                    for n in range(2):
                        ts = slice((2 * j + n) * 128, (2 * j + n) * 128 + 128)
                        last = mm3(e, bk[:, n * 256:n * 256 + 256],
                                   [(OH[:, ts], wh), (OH[:, ts], wlo), (OL[:, ts], wh)])
                    return last
                p = PE.do(mms, box["t"], box["o"], ready)
                sl["free"][s] = p
                oh_free[0] = p
                xs = X[:, b, 2 * j:2 * j + 2, :].rearrange("p t c -> p (t c)")
                d = DV.do(lambda e: e.tensor_tensor(xs, xs, bk[:, :], ALU.add), p, x_tok[b], x_prev.get((b, j)))
                x_prev[b, j] = d
                free(i, d)

            def mk(j):
                def f():
                    if j < 0:
                        start()
                    else:
                        piece(j)
                return f
            return [mk(j) for j in range(-1, 4)]

        x_prev = {}

        def norm(b):
            src = [x_prev[b, j] for j in range(4)]
            ss = [DV.do(lambda e, t=t: e.bn_stats(st[:, t, :], X[:, b, t, :]), src) for t in range(NT)]
            aa = [DV.do(lambda e, t=t: e.bn_aggr(mv[:, t, :], st[:, t, :]), ss[t]) for t in range(NT)]
            a = PO.do(lambda e: e.tensor_scalar(rs[:, :], mv[:, :, 1], EPS, None, ALU.add), aa)
            a = PO.do(lambda e: e.tensor_tensor(rs[:, :], rs[:, :], half[:, :], ALU.pow), a, k_half)
            d = [DV.do(lambda e, t=t: e.tensor_scalar(X[:, b, t, :], X[:, b, t, :], mv[:, t, 0:1], rs[:, t:t + 1],
                                                      ALU.subtract, ALU.mult), a) for t in range(NT)]
            x_tok[b] = d[-1]
            for j in range(4):
                x_prev[b, j] = d[-1]
            return d

        def transpose_x(b):
            pieces = []
            toks = []

            def piece(kt, c):
                bk, ready, i = take()

                def mms(e):
                    for n in range(4):
                        last = e.transpose(bk[:, n * 128:n * 128 + 128],
                                           X[:, b, 4 * c + n, kt * 128:kt * 128 + 128], idF[:, :])
                    return last
                p = PE.do(mms, x_tok[b], ld_cst, ready)
                h = XH[:, kt, c * 512:c * 512 + 512]
                l = XL[:, kt, c * 512:c * 512 + 512]
                a = AC.do(lambda e: e.activation(h, bk[:, :], ACT.Copy), p, xh_free[0])
                d = DV.do(lambda e: e.tensor_tensor(l, bk[:, :], h.bitcast(F), ALU.subtract), a, xh_free[0])
                free(i, d)
                toks.append(a)
                toks.append(d)
                if len(toks) == 8:
                    xh_tok[0] = list(toks)
            for kt in range(2):
                for c in range(2):
                    pieces.append(lambda kt=kt, c=c: piece(kt, c))
            return pieces

        units = [("self", 0), ("self", 1), ("cross", 0), ("cross", 1)]
        uidx = {u: n for n, u in enumerate(units)}
        ctx_tok = [None]

        for b in range(NB):
            d = [DV.do(lambda e, t=t, b=b: e.tensor_tensor(X[:, b, t, :], X[:, b, t, :], boS[:, :], ALU.add),
                       ld_x[b], ld_bo) for t in range(NT)]
            x_tok[b] = d[-1]

        def load_ctx():
            z = PO.do(lambda e: e.memset(SH[1][:, :], 0.0), tmp_free[1])
            cv_ = SH[1][:, 0:NB * 2 * LP].rearrange("p (b k n) -> p b k n", b=NB, k=2)
            for b in range(NB):
                for k in range(2):
                    t = load("ctx", cv_[:, b, k, 0:L], cT[b, k * 128:k * 128 + 128, :], z)
            a = PO.do(lambda e: e.tensor_copy(CH[:, :, :, :], cv_), t, z)
            d = PO.do(lambda e: e.tensor_tensor(CL[:, :, :, :], cv_, CH[:, :, :, :].bitcast(F), ALU.subtract), a)
            tmp_free[1] = [tmp_free[1], d]
            ctx_tok[0] = d

        load_ctx()

        stream = [(u, h) for u in units for h in range(NH)]
        for f in vgroup(units[0], 0) + prep(units[0], 0):
            f()
        mx, rows = maxima(*stream[0])
        for f in mx:
            f()
        rows()

        for n, (u, h) in enumerate(stream):
            kind, b = u
            pair, par = h // 2, h % 2
            ui = uidx[u]
            nblk = 12 if kind == "self" else 2
            work = []
            nxt = stream[n + 1] if n + 1 < len(stream) else None
            mx, rows = maxima(*nxt) if nxt else ([], None)
            if par == 0:
                nu, npair = (u, pair + 1) if pair + 1 < NP else (units[ui + 1] if ui + 1 < 4 else None, 0)
                if nu and npair == 0:
                    if nu == ("self", 1):
                        work.append(lambda: load_xT(1))
                    else:
                        work += transpose_x(nu[1])
                        if nu == ("cross", 0):
                            work.append(lambda: (load_w("wq1", 0, cq), load_w("wk1", 1, ck), load_w("wv1", 2, cv)))
                if nu:
                    work += prep(nu, npair)
                op = (u, pair - 1) if pair else (units[ui - 1], NP - 1) if ui else None
                if op:
                    first, *others = outproj(*op)
                    first()
                    work += others
                    if pair == 0:
                        work.append(lambda ob=op[0]: norm(ob[1]))
                        if op[0] == ("self", 1):
                            work.append(lambda: load_w("wo1", 3, co))
            elif pair % 2:
                g = pair // 2
                nu, ng = (u, g + 1) if g < 3 else (units[ui + 1] if ui + 1 < 4 else None, 0)
                if nu:
                    work += vgroup(nu, ng)
            if u == ("cross", 0) and h == 0:
                p_zero += [DV.do(lambda e, i=i: e.memset(PT[i][64:128, :], 0.0), P_free[i]) for i in range(3)]

            lead = mx if par == 0 else mx
            jobs = (lead + work) if par == 1 or True else work
            slots = [[] for _ in range(nblk)]
            per = len(mx) + len(work)
            mspan = max(1, (nblk * 3) // 4)
            for k, f in enumerate(mx):
                slots[k * mspan // max(1, len(mx))].append(f)
            for k, f in enumerate(work):
                slots[k * nblk // max(1, len(work))].append(f)
            if rows:
                slots[nblk - 1].append(rows)

            def fill(i, slots=slots):
                for f in slots[i]:
                    f()
            attend(u, h, fill)

        for f in outproj(units[3], NP - 1):
            f()
        norm(1)

        ff_ready = [set_free[p, q] for p in range(2) for q in range(2)]
        tW1 = load("W1", Wraw[0][:, :], W1, raw_free[0])
        tW2 = load("W2", Wraw[2][:, :], W2, raw_free[2])
        tb2 = load("b2", boS[:, :], b2, x_tok[0], x_tok[1])
        WH = [REG[:, 8192 + 2048 * i:8192 + 2048 * i + 2048] for i in range(4)]
        a1 = PO.do(lambda e: e.tensor_copy(WH[0], Wraw[0][:, :]), tW1, ff_ready)
        l1 = PO.do(lambda e: e.tensor_tensor(WH[1], Wraw[0][:, :], WH[0].bitcast(F), ALU.subtract), a1)
        a2 = PO.do(lambda e: e.tensor_copy(WH[2], Wraw[2][:, :]), tW2, ff_ready)
        l2 = PO.do(lambda e: e.tensor_tensor(WH[3], Wraw[2][:, :], WH[2].bitcast(F), ALU.subtract), a2)
        w1h, w1l = (w.rearrange("p (k n) -> p k n", k=2) for w in WH[0:2])
        w2h, w2l = (w.rearrange("p (k n) -> p k n", k=8) for w in WH[2:4])
        NC4 = 256
        HH = [REG[:, 4096 * i:4096 * i + 2048].rearrange("p (k n) -> p k n", k=8) for i in range(2)]
        HL = [REG[:, 4096 * i + 2048:4096 * i + 4096].rearrange("p (k n) -> p k n", k=8) for i in range(2)]
        h_free = [None] * 2
        hf_free = [None] * 2
        blend_tok = [P_free, None]
        router = {}

        def route(b):
            dd = []
            for t in range(NT):
                tmp = OF[:, 0:C]
                a = DV.do(lambda e, t=t: e.tensor_tensor(tmp, X[:, b, t, :], wrS[:, :], ALU.mult),
                          x_tok[b], ld_sm, of_free[0], dd[-1] if dd else None)
                dd.append(DV.do(lambda e, t=t: e.tensor_reduce(wl[:, t:t + 1], tmp, AX.X, ALU.add), a,
                                router.get("wl")))
            a = DV.do(lambda e: e.tensor_scalar(wl[:, :], wl[:, :], brS[:, 0:1], None, ALU.add), dd)
            cc = []

            def count(j):
                bk, ready, i = take()
                for n in range(4):
                    t = 4 * j + n
                    wb = OF[:, 256 + 128 * (n % 2):384 + 128 * (n % 2)]
                    c = DV.do(lambda e, t=t, wb=wb: e.tensor_copy(wb, wl[:, t:t + 1].to_broadcast([128, 128])),
                              a, router.get(n % 2))
                    ps = PE.do(lambda e, n=n, wb=wb: e.transpose(bk[:, n * 128:n * 128 + 128], wb, idF[:, :]),
                               c, ready)
                    router[n % 2] = ps
                for t in range(NT):
                    k = DV.do(lambda e, t=t: e.tensor_scalar(
                        OF[:, 512:1024], bk[:, :], wl[:, t:t + 1], None, ALU.is_ge, ALU.add,
                        accum_out=cnt[:, t, j:j + 1]), ps, router.get("sel"), cc[-1] if cc else None)
                    cc.append(k)
                free(i, k)
            count(0)
            count(1)
            a = DV.do(lambda e: e.tensor_tensor(cnt[:, :, 0], cnt[:, :, 0], cnt[:, :, 1], ALU.add), cc)
            router["wl"] = a
            return DV.do(lambda e: e.tensor_scalar(sel[:, :], cnt[:, :, 0], TOP - 0.5, None, ALU.is_lt),
                         a, router.get("blend"))

        def hidden(b, q):
            i2 = (b * 4 + q) % 2
            qs = slice(q * NC4, q * NC4 + NC4)
            toks = []

            def tile(m):
                bk, ready, i = take()

                def mms(e):
                    for n in range(2):
                        hs = slice((2 * m + n) * 128, (2 * m + n) * 128 + 128)
                        terms = []
                        for k in range(2):
                            terms += [(w1h[:, k, hs], XH[:, k, qs]), (w1h[:, k, hs], XL[:, k, qs]),
                                      (w1l[:, k, hs], XH[:, k, qs])]
                        last = mm3(e, bk[:, n * 256:n * 256 + 256], terms)
                    return last
                p = PE.do(mms, xh_tok[0], l1, ready)
                xh_free[0] = p
                j = m % 2
                for n in range(2):
                    g = AC.do(lambda e, n=n, j=j: e.activation(
                        T1[j][:, n * 256:n * 256 + 256], bk[:, n * 256:n * 256 + 256], ACT.Gelu,
                        bias=b1S[:, 2 * m + n:2 * m + n + 1], scale=1.0), p, ld_sm, tmp_free[j])
                free(i, g)
                hh = HH[i2][:, 2 * m:2 * m + 2, :].rearrange("p k n -> p (k n)")
                hl = HL[i2][:, 2 * m:2 * m + 2, :].rearrange("p k n -> p (k n)")
                a = DV.do(lambda e, j=j, hh=hh: e.tensor_copy(hh, T1[j][:, :]), g, h_free[i2], ff_ready)
                d = DV.do(lambda e, j=j, hh=hh, hl=hl: e.tensor_tensor(hl, T1[j][:, :], hh.bitcast(F),
                                                                       ALU.subtract), a)
                tmp_free[j] = d
                toks.extend([a, d])
            for m in range(4):
                tile(m)
            return toks

        def finish(b, q, toks, sl_tok):
            i2 = (b * 4 + q) % 2
            bk, ready, i = take()

            def mms(e):
                for n in range(2):
                    ts = slice(n * 128, n * 128 + 128)
                    terms = []
                    for k in range(8):
                        terms += [(HH[i2][:, k, ts], w2h[:, k, :]), (HH[i2][:, k, ts], w2l[:, k, :]),
                                  (HL[i2][:, k, ts], w2h[:, k, :])]
                    last = mm3(e, bk[:, n * 256:n * 256 + 256], terms)
                return last
            p = PE.do(mms, toks, l2, ready)
            h_free[i2] = p
            for n in range(2):
                t = 2 * q + n
                xs = X[:, b, t, :]
                y = PT[n][:, 0:256]
                a = DV.do(lambda e, n=n, y=y: e.tensor_tensor(y, bk[:, n * 256:n * 256 + 256], boS[:, :], ALU.add),
                          p, tb2, P_free[n], router.get(("y", n)))
                z = DV.do(lambda e, t=t, xs=xs: e.tensor_scalar(xs, xs, nsel[:, t:t + 1], None, ALU.mult),
                          sl_tok, x_tok[b])
                d = DV.do(lambda e, t=t, xs=xs, y=y: e.scalar_tensor_tensor(xs, y, sel[:, t:t + 1], xs,
                                                                            ALU.mult, ALU.add), a, z)
                router["y", n] = d
                x_prev[b, t // 2] = d
            free(i, a)
            router["blend"] = d

        nsel = sb("nsel", [128, NT])
        outs = []
        for b in range(NB):
            for f in transpose_x(b):
                f()
            s = route(b)
            sl_tok = [s, DV.do(lambda e: e.tensor_scalar(nsel[:, :], sel[:, :], -1.0, 2.0, ALU.mult, ALU.add),
                               s, router.get("blend"))]
            prev = None
            for q in range(4):
                tk = hidden(b, q)
                if prev:
                    finish(b, *prev, sl_tok)
                prev = (q, tk)
            finish(b, *prev, sl_tok)
            d = norm(b)
            outs.append(load("out", out[b].rearrange("(n p) c -> p n c", p=128), X[:, b, :, :], d))
        SP.wait(*outs)

        @block.sync
        def _(e):
            SP.run(e)

        @block.scalar
        def _(e):
            AC.run(e)

        @block.vector
        def _(e):
            DV.run(e)

        @block.gpsimd
        def _(e):
            PO.run(e)

        @block.tensor
        def _(e):
            PE.run(e)


def kernel(**inputs):
    import numpy as np
    import concourse.bacc as _bacc
    from concourse import mybir as _mybir
    from concourse.bass_utils import run_bass_kernel_spmd as _run

    g = {k: np.asarray(v) for k, v in inputs.items()}

    def rows(w, k):
        return w.reshape(k, 128, -1).transpose(1, 0, 2).reshape(128, -1)

    inv = (1.0 / np.float32(10000.0) ** (np.arange(0, D, 2, dtype=np.float32) / np.float32(D))).astype(np.float32)
    ang = np.arange(T, dtype=np.float32)[:, None] * inv[None, :]
    sn, cs = np.sin(ang).astype(np.float32), np.cos(ang).astype(np.float32)
    cosT = np.tile(np.repeat(cs.T, 2, axis=0), (2, 1))
    sinT = np.repeat(sn.T, 2, axis=0)
    sinT[0::2] = -sinT[0::2]
    sinT = np.tile(sinT, (2, 1))
    i = np.arange(128)
    feed = {
        "xT": g["x"].transpose(0, 2, 1), "x": g["x"], "cT": g["ctx_1024"].transpose(0, 2, 1),
        "Wq": rows(g["L0_attn_Wq"], 2), "Wk": rows(g["L0_attn_Wk"], 2), "Wv": rows(g["L0_attn_Wv"], 2),
        "Wo": rows(g["L0_attn_Wo"], 8), "bo": np.tile(g["L0_attn_bo"][None], (128, 1)),
        "cq": rows(g["L0_xattn_w_q"], 2), "ck": rows(g["L0_xattn_w_k"], 2), "cv": rows(g["L0_xattn_w_v"], 2),
        "co": rows(g["L0_xattn_w_o"], 8), "wr": np.tile(g["L0_ffn_w_r"].reshape(1, -1), (128, 1)),
        "br": np.tile(g["L0_ffn_b_r"].reshape(1, 1), (128, 1)),
        "W1": rows(g["L0_ffn_W1"], 2), "b1": g["L0_ffn_b1"].reshape(8, 128).T,
        "W2": rows(g["L0_ffn_W2"], 8), "b2": np.tile(g["L0_ffn_b2"][None], (128, 1)),
        "cosT": cosT, "sinT": sinT, "identd": np.eye(128, dtype=np.float32),
        "maskqk": np.where(i[None, :] > i[:, None], np.float32(NEG), np.float32(0)),
        "maskkq": np.where(i[None, :] < i[:, None], np.float32(NEG), np.float32(0)),
    }
    nc = _bacc.Bacc("TRN2", target_bir_lowering=False, num_devices=1)
    arrays, args = {}, []
    for name, a in feed.items():
        a = np.ascontiguousarray(a)
        arrays["in_" + name] = a
        args.append(nc.dram_tensor("in_" + name, a.shape, _mybir.dt.from_np(a.dtype), kind="ExternalInput").ap())
    args.append(nc.dram_tensor("out_0", (NB, T, C), _mybir.dt.float32, kind="ExternalOutput").ap())
    build(nc, *args)
    r = _run(nc, [arrays], core_ids=[0])
    return r.results[0]["out_0"]
```

```python
import concourse.bass as bass
from concourse import mybir
from contextlib import ExitStack

F = mybir.dt.float32
R = mybir.dt.float32r
BF = mybir.dt.bfloat16
ALU = mybir.AluOpType
ACT = mybir.ActivationFunctionType
AX = mybir.AxisListType

NB, T, C, NH, D = 2, 1024, 256, 16, 64
L = 77
LP = 78
NP = NH // 2
NT = T // 128
TOP = 512
NEG = -1.0e30
EPS = 1e-5
SWAP = [i ^ 1 for i in range(32)]


class Engine:

    def __init__(self, sem):
        self.sem, self.count, self.queue, self.seen = sem, 0, [], {}

    def wait(self, *tokens):
        for tok in tokens:
            if tok is None:
                continue
            if isinstance(tok, list):
                self.wait(*tok)
                continue
            sem, value = tok
            if self.seen.get(sem, 0) < value:
                self.seen[sem] = value
                self.queue.append(lambda e, s=sem, v=value: e.wait_ge(s, v))

    def do(self, fn, *waits):
        self.wait(*waits)
        self.count += 1
        self.queue.append(lambda e: fn(e).then_inc(self.sem, 1))
        return (self.sem, self.count)

    def run(self, e):
        for f in self.queue:
            f(e)


def build(nc, xT, x, cT, Wq, Wk, Wv, Wo, bo, cq, ck, cv, co, wr, br, W1, b1, W2, b2, cosT, sinT,
          identd, maskqk, out):
    ctx = ExitStack()
    with ctx:
        def sb(name, shape, dt=F):
            return ctx.enter_context(nc.sbuf_tensor(name, shape, dt))

        def sem(name):
            return ctx.enter_context(nc.semaphore(name))

        PE, AC, DV, PO, SP = (Engine(sem(n)) for n in ("s_pe", "s_act", "s_dve", "s_pool", "s_sp"))
        dma_sems = {}

        def load(name, dst, src, *waits):
            SP.wait(*waits)
            if name not in dma_sems:
                dma_sems[name] = [sem("d_" + name), 0]
            d = dma_sems[name]
            d[1] += 16
            SP.queue.append(lambda e: e.dma_start(dst, src).then_inc(d[0], 16))
            return (d[0], d[1])

        Wraw = [sb(f"Wraw{i}", [128, 2048]) for i in range(4)]
        SLH = [sb(f"SLH{i}", [128, 512], R) for i in range(2)]
        SLL = [sb(f"SLL{i}", [128, 512], R) for i in range(2)]
        REG = sb("REG", [128, 16384], R)
        XH = sb("XH", [128, 2, T], R)
        XL = sb("XL", [128, 2, T], R)
        VV = [sb(f"VV{i}", [128, NT, 384]) for i in range(2)]
        OH = sb("OH", [128, T], R)
        OL = sb("OL", [128, T], R)
        NU = [sb(f"NU{i}", [128, T]) for i in range(2)]
        RBC = [sb(f"RBC{i}", [128, 512]) for i in range(2)]
        DR = sb("DR", [128, 512])
        RCP = [sb(f"RCP{i}", [128, 4, 4]) for i in range(2)]
        X = sb("X", [128, NB, NT, C])
        PT = [sb(f"PT{i}", [128, 512]) for i in range(3)]
        cosS = sb("cosS", [128, T])
        sinS = sb("sinS", [128, T])
        T1 = [sb(f"T1{i}", [128, 512]) for i in range(2)]
        SH = [sb(f"SH{i}", [128, 512]) for i in range(2)]
        NM = [sb(f"NM{i}", [128, 16]) for i in range(2)]
        MH = [sb(f"MH{i}", [16, 128], R) for i in range(2)]
        ML = [sb(f"ML{i}", [16, 128], R) for i in range(2)]
        idF = sb("idF", [128, 128])
        idB = sb("idB", [128, 128], BF)
        mQK = sb("mQK", [128, 128], BF)
        boS = NU[1][:, 0:C]
        b2S = cosS[:, C:2 * C]
        wrS = cosS[:, 0:C]
        b1S = sb("b1S", [128, NT])
        brS = sb("brS", [128, 1])
        st = sb("st", [128, NT, 6])
        mv = sb("mv", [128, NT, 2])
        rs = sb("rs", [128, NT])
        half = sb("half", [128, NT])
        wl = sb("wl", [128, NT])
        cnt = sb("cnt", [128, NT, 2])
        sel = sb("sel", [128, NT])

        bank = [ctx.enter_context(nc.psum_tensor(f"bank{i}", [128, 512], F)) for i in range(8)]
        ST, OB, RB = bank[0:2], bank[2:4], bank[4:8]
        block = ctx.enter_context(nc.Block())

        def setview(kind, par, buf):
            o = ((par * 2 + buf) * 4 + kind) * 1024
            return REG[:, o:o + 1024]

        CH, CL = (REG[:, 3072 + 512 * n:3072 + 512 * n + NB * 2 * LP].rearrange(
            "p (b k n) -> p b k n", b=NB, k=2) for n in range(2))
        XQ = [0, 4, 6]

        def view(u, pair, par, kind):
            if u[0] == "self":
                return setview(kind, par, (uidx[u] * NP + pair) % 2)
            bf = ((uidx[u] - 2) * NP + pair) % 3
            if kind < 2:
                o = (8 * par + XQ[bf] + kind) * 1024
                return REG[:, o:o + 1024]
            o = 2048 + ((bf * 2 + par) * 2 + kind - 2) * LP
            return REG[:, o:o + LP]

        def setkey(u, pair, par):
            return (par, (uidx[u] % 2 * NP + pair) % (2 if u[0] == "self" else 3))

        units = [("self", 0), ("self", 1), ("cross", 0), ("cross", 1)]
        uidx = {u: n for n, u in enumerate(units)}

        ring = [(n, None) for n in range(4)]

        def take():
            i, tok = ring.pop(0)
            return RB[i], tok, i

        def free(i, tok):
            ring.append((i, tok))

        raw_free = [None] * 4
        raw_tok = {}

        def load_w(key, slot, ap):
            raw_tok[key] = load(key, Wraw[slot][:, :], ap, raw_free[slot])

        stage = {"free": [None] * 2, "n": 0}
        tmp_free = [None] * 2

        ld_cst = load("cst", idF[:, :], identd)
        mtmp = load("msk", T1[0][:, 0:128], maskqk)
        load_w("wv0", 2, Wv)
        xT_ready = {}

        k_idb = AC.do(lambda e: e.activation(idB[:, :], idF[:, :], ACT.Copy), ld_cst)
        k_mqk = AC.do(lambda e: e.activation(mQK[:, :], T1[0][:, 0:128], ACT.Copy), mtmp)
        k_cst = [k_idb, k_mqk]
        tmp_free[0] = k_mqk

        xh_free = [None]
        xh_tok = [None]
        tn = [0]

        def load_xT(b):
            toks = []
            for j in range(4):
                i = tn[0] % 2
                tn[0] += 1
                kt, c = j // 2, j % 2
                t = load(f"xT{i}", T1[i][:, :], xT[b, kt * 128:kt * 128 + 128, c * 512:c * 512 + 512],
                         tmp_free[i])
                h = XH[:, kt, c * 512:c * 512 + 512]
                l = XL[:, kt, c * 512:c * 512 + 512]
                a = AC.do(lambda e, h=h, i=i: e.activation(h, T1[i][:, :], ACT.Copy), t, xh_free[0])
                d = DV.do(lambda e, h=h, l=l, i=i: e.tensor_tensor(l, T1[i][:, :], h.bitcast(F), ALU.subtract),
                          a, t, xh_free[0])
                tmp_free[i] = d
                toks += [a, d]
            xh_tok[0] = toks

        load_xT(0)
        load_w("wq0", 0, Wq)
        load_w("wk0", 1, Wk)
        ld_rope = load("rope", cosS[:, :], cosT)
        ld_rope = load("rope", sinS[:, :], sinT)
        load_w("wo0", 3, Wo)
        ld_x = [load(f"x{b}", X[:, b, :, :], x[b].rearrange("(n p) c -> p n c", p=128)) for b in range(NB)]
        ld_bo = load("bo", boS, bo)
        ld_sm = load("sm", b1S[:, :], b1)
        ld_sm = load("sm", brS[:, :], br)

        k_ones = [PO.do(lambda e, v=v: e.memset(
            v[:, :, :].rearrange("p t (a s d) -> p t a s d", a=2, s=3)[:, :, :, 1, :], 1.0)) for v in VV]
        k_half = PO.do(lambda e: e.memset(half[:, :], -0.5))
        k_aug = {}
        z = k_half
        for par in range(2):
            for buf in range(2):
                aug = 64 * (1 - par)
                q2, k2 = setview(1, par, buf), setview(3, par, buf)
                z = PO.do(lambda e, a=q2[aug:aug + 64, :].bitcast(F): e.memset(a, 0.0), z)
                z = PO.do(lambda e, a=k2[aug:aug + 64, :].bitcast(F): e.memset(a, 0.0), z)
                z = PO.do(lambda e, a=k2[aug:aug + 2, :].bitcast(F): e.memset(a, 1.0), z)
            k_aug[par] = z
        PO.wait(z)

        sl = {"n": 0, "free": [None] * 2}

        def split(parts, key):
            i = sl["n"] % 2
            sl["n"] += 1
            o, toks = 0, []
            for raw, slot, tok in parts:
                shp = raw.shape[1:]
                n = 1
                for s in shp:
                    n *= s
                h, l = SLH[i][:, o:o + n], SLL[i][:, o:o + n]
                if len(shp) == 2:
                    h = h.rearrange("p (a b) -> p a b", a=shp[0])
                    l = l.rearrange("p (a b) -> p a b", a=shp[0])
                a = PO.do(lambda e, h=h, r=raw: e.tensor_copy(h, r), tok, sl["free"][i])
                d = PO.do(lambda e, h=h, l=l, r=raw: e.tensor_tensor(l, r, h.bitcast(F), ALU.subtract),
                          a, sl["free"][i])
                raw_free[slot] = d
                toks.append(d)
                o += n
            return i, toks[-1]

        def wview(slot):
            return Wraw[slot][:, :].rearrange("p (k n) -> p k n", k=2)

        def woview(slot):
            return Wraw[slot][:, :].rearrange("p (k n) -> p k n", k=8)

        def mm3(e, o, terms):
            for n, (a, b) in enumerate(terms):
                last = e.matmul(o, a, b, start=n == 0, stop=n == len(terms) - 1)
            return last

        set_free = {}
        rope_last = []
        set_tok = {}
        P_free = [None] * 3

        def x_wait(u, pair):
            if u == units[2] and pair < 3:
                return [t for k, ts in set_free.items() if k[0] == "self" and (pair or k[2] == 0) for t in ts]
            return []

        def prep(u, pair):
            kind, b = u
            key = "0" if kind == "self" else "1"
            pc = slice(pair * 128, pair * 128 + 128)
            pieces = []
            box = {}

            def start():
                box["s"], box["t"] = split([(wview(0)[:, :, pc], 0, raw_tok["wq" + key]),
                                            (wview(1)[:, :, pc], 1, raw_tok["wk" + key])], key)
                for par in range(2):
                    set_tok[u, pair, par] = [k_aug[par] if kind == "self" else k_aug["x"]]

            def proj(which, c):
                s = box["s"]
                wh = SLH[s][:, which * 256:which * 256 + 256].rearrange("p (k n) -> p k n", k=2)
                wlo = SLL[s][:, which * 256:which * 256 + 256].rearrange("p (k n) -> p k n", k=2)
                if kind == "self" or which == 0:
                    w = 512
                    xh = [XH[:, k, c * 512:c * 512 + 512] for k in range(2)]
                    xl = [XL[:, k, c * 512:c * 512 + 512] for k in range(2)]
                    dep = xh_tok[0]
                else:
                    w = LP
                    xh = [CH[:, b, k, :] for k in range(2)]
                    xl = [CL[:, b, k, :] for k in range(2)]
                    dep = ctx_tok[0]
                bk, ready, i = take()
                terms = []
                for k in range(2):
                    terms += [(wh[:, k, :], xh[k]), (wh[:, k, :], xl[k]), (wlo[:, k, :], xh[k])]
                p = PE.do(lambda e: mm3(e, bk[:, 0:w], terms), box["t"], dep, ready)
                sl["free"][s] = p
                if kind == "self" or which == 0:
                    xh_free[0] = p
                cs = slice(c * 512, c * 512 + w)
                j = tn[0] % 2
                if kind == "self":
                    tn[0] += 1
                    a = DV.do(lambda e: e.tensor_tensor(T1[j][:, :], bk[:, :], cosS[:, cs], ALU.mult),
                              p, ld_rope, tmp_free[j])
                    d = DV.do(lambda e: e.stream_shuffle(SH[j][:, :], bk[:, :], SWAP))
                    free(i, d)
                    rope_last[:] = [a]
                    g = PO.do(lambda e: e.tensor_tensor(SH[j][:, :], SH[j][:, :], sinS[:, cs], ALU.mult),
                              d, ld_rope)
                    g = PO.do(lambda e: e.tensor_tensor(T1[j][:, :], T1[j][:, :], SH[j][:, :], ALU.add),
                              g, a)
                    src, dep2 = T1[j][:, :], g
                else:
                    src, dep2 = bk[:, 0:w], p
                def parts():
                    store(which, w, cs, src, dep2, i, j)
                return parts

            def store(which, w, cs, src, dep2, i, j):
                hi = []
                frees = [set_free.get((u[0], *setkey(u, pair, par)), []) + x_wait(u, pair) for par in range(2)]
                for par in range(2):
                    base = 64 * par
                    t = view(u, pair, par, 0 if which == 0 else 2)[base:base + 64, cs]
                    hi.append(AC.do(lambda e, t=t, s=src[base:base + 64, :]: e.activation(t, s, ACT.Copy),
                                    dep2, frees[par]))
                lo = []
                for par in range(2):
                    base, aug = 64 * par, 64 * (1 - par)
                    t = view(u, pair, par, 0 if which == 0 else 2)[base:base + 64, cs]
                    l = (view(u, pair, par, 0)[aug:aug + 64, cs] if which == 0
                         else view(u, pair, par, 3)[base:base + 64, cs])
                    on = PO if kind == "self" and which == 1 else DV
                    if on is PO and par:
                        PO.wait((PO.sem, PO.count))
                    lo.append(on.do(lambda e, t=t, l=l, s=src[base:base + 64, :]: e.tensor_tensor(
                        l, s, t.bitcast(F), ALU.subtract), hi, dep2, frees[par]))
                if kind == "self":
                    tmp_free[j] = lo
                    if which == 1:
                        PO.wait(lo[-1])
                else:
                    free(i, lo[-1])
                for par in range(2):
                    base, aug = 64 * par, 64 * (1 - par)
                    t = view(u, pair, par, 0 if which == 0 else 2)[base:base + 64, cs]
                    dup = (view(u, pair, par, 1)[base:base + 64, cs] if which == 0
                           else view(u, pair, par, 2)[aug:aug + 64, cs])
                    k = load(f"dup{which}{par}", dup.bitcast(F), t.bitcast(F), hi[par], frees[par])
                    set_tok[u, pair, par] += [k, lo[par]]

            order = [(1, 0), (0, 0), (1, 1), (0, 1)] if kind == "self" else [(1, 0), (0, 0), (0, 1)]
            later = {}

            def first(n, w_, c_):
                later[n] = proj(w_, c_)
            return (start, [lambda n=n, w_=w_, c_=c_: first(n, w_, c_) for n, (w_, c_) in enumerate(order)],
                    [lambda n=n: later[n]() for n in range(len(order))])

        vv_free = [None] * 2
        vv_tok = {}

        def vgroup(u, g):
            kind, b = u
            v = (uidx[u] * 4 + g) % 2 if kind == "self" else uidx[u] % 2
            key = "0" if kind == "self" else "1"
            box = {}

            def start():
                box["s"], box["t"] = split([(wview(2)[:, :, g * 256:g * 256 + 256], 2, raw_tok["wv" + key])], key)
                vv_tok[u, g] = [k_ones[v]]

            def piece(j):
                s = box["s"]
                wh = SLH[s][:, :].rearrange("p (k n) -> p k n", k=2)
                wlo = SLL[s][:, :].rearrange("p (k n) -> p k n", k=2)
                bk, ready, i = take()
                tiles = [2 * j, 2 * j + 1] if kind == "self" else [0]
                rows = 128 if kind == "self" else L

                def mms(e):
                    for n, t in enumerate(tiles):
                        if kind == "self":
                            xh = [XH[:, k, t * 128:t * 128 + 128] for k in range(2)]
                            xl = [XL[:, k, t * 128:t * 128 + 128] for k in range(2)]
                        else:
                            xh = [CH[:, b, k, 0:L] for k in range(2)]
                            xl = [CL[:, b, k, 0:L] for k in range(2)]
                        terms = []
                        for k in range(2):
                            terms += [(xh[k], wh[:, k, :]), (xh[k], wlo[:, k, :]), (xl[k], wh[:, k, :])]
                        last = mm3(e, bk[0:rows, n * 256:n * 256 + 256], terms)
                    return last
                p = PE.do(mms, box["t"], xh_tok[0] if kind == "self" else ctx_tok[0], ready)
                sl["free"][s] = p
                if kind == "self":
                    xh_free[0] = p
                for n, t in enumerate(tiles):
                    dst = VV[v][0:rows, t if kind == "self" else g, :].rearrange("p (a s d) -> p a s d", a=2, s=3)[:, :, 0:3:2, :]
                    src = bk[0:rows, n * 256:n * 256 + 256].rearrange("p (a s d) -> p a s d", a=2, s=2)
                    k = AC.do(lambda e, dst=dst, src=src: e.activation(dst, src, ACT.Copy), p, vv_free[v])
                free(i, k)
                vv_tok[u, g].append(k)

            n = 4 if kind == "self" else 1

            return start, [lambda j=j: piece(j) for j in range(n)]

        nm_free = [None] * 2
        mh_free = [None] * 2

        def max_self(u, h):
            pair, par = h // 2, h % 2
            q1, k1 = view(u, pair, par, 0), view(u, pair, par, 2)
            m = h % 2
            toks = []

            def chunk(qt, kc):
                k0 = kc * 512
                w = min(512, (qt + 1) * 128 - k0)
                diag = (qt + 1) * 128 <= k0 + 512
                col = qt if kc == 0 else 4 + qt
                bk, ready, i = take()

                def mms(e):
                    last = e.matmul(bk[:, 0:w], q1[:, qt * 128:qt * 128 + 128], k1[:, k0:k0 + w],
                                    start=True, stop=not diag)
                    if diag:
                        last = e.matmul(bk[:, w - 128:w], idB[:, :], mQK[:, :], start=False, stop=True)
                    return last
                p = PE.do(mms, set_tok[u, pair, par], k_cst, ready)
                d = DV.do(lambda e: e.tensor_reduce(NM[m][:, col:col + 1], bk[:, 0:w], AX.X, ALU.max,
                                                    negate=True), p, nm_free[m])
                free(i, d)
                toks.append(d)

            box = {}

            def least():
                box["d"] = DV.do(lambda e: e.tensor_tensor(NM[m][:, 4:8], NM[m][:, 4:8], NM[m][:, 8:12], ALU.min),
                                 toks)

            def turn():
                box["f"] = to_rows(u, m, 8, box["d"], [(pair, par)])
            order = [(qt, kc) for qt in range(NT) for kc in range(qt // 4 + 1)]
            return [lambda qt=qt, kc=kc: chunk(qt, kc) for qt, kc in order], least, turn, lambda: box["f"]()

        def to_rows(u, m, n, dep, heads):
            bk, ready, i = take()
            p = PE.do(lambda e: e.transpose(bk[0:n, 0:128], NM[m][:, 0:n], idF[:, :]), dep, ld_cst, ready)
            nm_free[m] = p

            def f():
                rows_of(u, m, n, heads, bk, i, p)
            return f

        def rows_of(u, m, n, heads, bk, i, p):
            a = DV.do(lambda e: e.tensor_copy(MH[m][0:n, :], bk[0:n, 0:128]), p, mh_free[m])
            d = DV.do(lambda e: e.tensor_tensor(ML[m][0:n, :], bk[0:n, 0:128], MH[m][0:n, :].bitcast(F),
                                                ALU.subtract), a, mh_free[m])
            free(i, d)
            mh_free[m] = []
            for k, (pair, par) in enumerate(heads):
                q2 = view(u, pair, par, 1)
                aug = 64 * (1 - par)
                for s, (src, dep2) in enumerate(((MH[m], a), (ML[m], d))):
                    t = load(f"rows{m}{k}", q2[aug + s:aug + s + 1, :].bitcast(F),
                             src[8 * k:8 * k + 8, :].bitcast(F), dep2,
                             set_free.get((u[0], *setkey(u, pair, par)), []) + x_wait(u, pair))
                    mh_free[m].append(t)
                set_tok[u, pair, par].append(t)

        def max_cross(u, pair):
            m = pair % 2
            toks = []

            def chunk(par, j):
                q1, k1 = view(u, pair, par, 0), view(u, pair, par, 2)
                bk, ready, i = take()

                def mms(e):
                    for n in range(4):
                        qt = 4 * j + n
                        last = e.matmul(bk[:, n * 128:n * 128 + LP], q1[:, qt * 128:qt * 128 + 128],
                                        k1[:, 0:LP], start=True, stop=True)
                    return last
                p = PE.do(mms, set_tok[u, pair, par], ready)
                c0 = 8 * par + 4 * j
                d = DV.do(lambda e: e.tensor_reduce(
                    NM[m][:, c0:c0 + 4], bk[:, :].rearrange("p (n k) -> p n k", n=4)[:, :, 0:L],
                    AX.X, ALU.max, negate=True), p, nm_free[m])
                free(i, d)
                toks.append(d)

            box = {}

            def turn():
                box["f"] = to_rows(u, m, 16, toks, [(pair, 0), (pair, 1)])
            return ([lambda par=par, j=j: chunk(par, j) for par in range(2) for j in range(2)],
                    lambda: None, turn, lambda: box["f"]())

        st_free = [None] * 2
        o_free = [None] * 2
        nu_free = [None] * 2
        dr_free = [DV.do(lambda e: e.memset(DR[:, :], 1.0))]
        rcp_free = [None] * 2
        rb_free = [None] * 2
        of_tok = {}
        sn, pn = [0], [0]
        x_tok = {}
        p_zero = []

        def scores(u, h, c, kt):
            kind = u[0]
            pair, par = h // 2, h % 2
            q1, q2, k1, k2 = (view(u, pair, par, n) for n in range(4))
            rows = 128 if kind == "self" else L
            q0 = max(kt * 128, c * 512) if kind == "self" else c * 512
            w = (c + 1) * 512 - q0
            s, i = sn[0] % 2, sn[0] % 3
            sn[0] += 1
            diag = kind == "self" and kt * 128 >= c * 512
            ks = slice(kt * 128, kt * 128 + rows)

            def mms(e):
                e.matmul(ST[s][0:rows, 0:w], k1[:, ks], q1[:, q0:q0 + w], start=True, stop=False)
                last = e.matmul(ST[s][0:rows, 0:w], k2[:, ks], q2[:, q0:q0 + w], start=False, stop=not diag)
                if diag:
                    last = e.matmul(ST[s][:, 0:128], mQK[:, :], idB[:, :], start=False, stop=True)
                return last
            p = PE.do(mms, set_tok[u, pair, par], st_free[s])
            ex = AC.do(lambda e: e.activation(PT[i][0:rows, 0:w], ST[s][0:rows, 0:w], ACT.Exp, scale=D ** -0.5),
                       p, P_free[i], p_zero if kind == "cross" else None)
            st_free[s] = ex
            set_free[(kind, *setkey(u, pair, par))] = [p]
            return (u, h, c, kt, q0, w, i, ex)

        def pv(u, h, c, kt, q0, w, i, ex):
            kind = u[0]
            pair, par = h // 2, h % 2
            g = pair // 2
            v = (uidx[u] * 4 + g) % 2 if kind == "self" else uidx[u] % 2
            vt = kt if kind == "self" else g
            vc = (pair % 2) * 192 + 64 * par
            base, den = 64 * par, 64 * (1 - par)
            first = kt == 0
            last_kt = kt == (4 * c + 3 if kind == "self" else 0)
            o0 = q0 - c * 512
            p = PE.do(lambda e: e.matmul(OB[c][:, o0:o0 + w], VV[v][:, vt, vc:vc + 128], PT[i][:, 0:w],
                                         start=first, stop=last_kt),
                      ex, vv_tok[u, g], o_free[c] if first else None)
            P_free[i] = p
            vv_free[v] = p
            if last_kt:
                nu = NU[pair % 2]
                row = 64 * par + 32 * c
                a = AC.do(lambda e: e.activation(nu[base:base + 64, c * 512:c * 512 + 512],
                                                 OB[c][base:base + 64, :], ACT.Copy), p, nu_free[pair % 2])
                d = AC.do(lambda e: e.activation(DR[row:row + 1, :], OB[c][den:den + 1, :], ACT.Copy), p, dr_free[0])
                o_free[c] = d
                of_tok.setdefault((u, pair), []).extend([a, d])

        oh_free = [None]

        def outproj(u, pair):
            kind, b = u
            key = "0" if kind == "self" else "1"
            box = {}

            nu, rc = NU[pair % 2], RCP[pair % 2]

            def weights():
                box["s"], box["t"] = split([(woview(3)[:, pair, :], 3, raw_tok["wo" + key])], key)

            def denoms():
                bk, ready, i = take()

                def mms(e):
                    for n in range(4):
                        last = e.transpose(bk[:, n * 128:n * 128 + 128], DR[:, n * 128:n * 128 + 128], idF[:, :])
                    return last
                p = PE.do(mms, of_tok[u, pair], ld_cst, ready)
                dr_free[0] = p
                d = DV.do(lambda e: e.reciprocal(
                    rc[:, :, :], bk[:, :].rearrange("p (n r s) -> p n r s", n=4, r=4)[:, :, :, 0]),
                    p, rcp_free[pair % 2])
                free(i, d)
                rcp_free[pair % 2] = []
                box["r"] = []
                for c in range(2):
                    w = rc[:, :, c:4:2].unsqueeze(3).to_broadcast([128, 4, 2, 64])
                    k = DV.do(lambda e, c=c, w=w: e.tensor_copy(
                        RBC[c][:, :].rearrange("p (n h m) -> p n h m", n=4, h=2), w), d, rb_free[c])
                    box["r"].append(k)
                    rcp_free[pair % 2].append(k)
                box["o"] = []

            def normalise(c):
                bk, ready, i = take()
                cs = slice(c * 512, c * 512 + 512)

                def mms(e):
                    for n in range(4):
                        last = e.transpose(bk[:, n * 128:n * 128 + 128], RBC[c][:, n * 128:n * 128 + 128],
                                           idF[:, :])
                    return last
                p = PE.do(mms, box["r"][c], ready)
                rb_free[c] = p
                d = DV.do(lambda e: e.tensor_tensor(nu[:, cs], bk[:, :], nu[:, cs], ALU.mult), p, of_tok[u, pair])
                free(i, d)
                a = AC.do(lambda e: e.activation(OH[:, cs], nu[:, cs], ACT.Copy), d, oh_free[0])
                g = PO.do(lambda e: e.tensor_tensor(OL[:, cs], nu[:, cs], OH[:, cs].bitcast(F), ALU.subtract),
                          a, oh_free[0])
                nu_free[pair % 2] = g
                box["o"] += [a, g]

            def piece(j):
                s = box["s"]
                bk, ready, i = take()
                wh, wlo = SLH[s][:, 0:256], SLL[s][:, 0:256]

                def mms(e):
                    for n in range(2):
                        ts = slice((2 * j + n) * 128, (2 * j + n) * 128 + 128)
                        last = mm3(e, bk[:, n * 256:n * 256 + 256],
                                   [(OH[:, ts], wh), (OH[:, ts], wlo), (OL[:, ts], wh)])
                    return last
                p = PE.do(mms, box["t"], box["o"], ready)
                sl["free"][s] = p
                oh_free[0] = p
                xs = X[:, b, 2 * j:2 * j + 2, :].rearrange("p t c -> p (t c)")
                d = DV.do(lambda e: e.tensor_tensor(xs, xs, bk[:, :], ALU.add), p, x_tok[b], x_prev.get((b, j)))
                x_prev[b, j] = d
                free(i, d)

            return [weights, denoms, lambda: normalise(0), lambda: normalise(1)] + [lambda j=j: piece(j) for j in range(4)]

        x_prev = {}
        ln_free = []

        def norm(b, tiles=range(NT)):
            src = [x_prev[b, t // 2] for t in tiles]
            t0, t1 = tiles[0], tiles[-1] + 1
            ss = [DV.do(lambda e, t=t: e.bn_stats(st[:, t, :], X[:, b, t, :]), src, ln_free) for t in tiles]
            aa = [DV.do(lambda e, t=t: e.bn_aggr(mv[:, t, :], st[:, t, :]), ss[n]) for n, t in enumerate(tiles)]
            a = PO.do(lambda e: e.tensor_scalar(rs[:, t0:t1], mv[:, t0:t1, 1], EPS, None, ALU.add), aa)
            a = PO.do(lambda e: e.tensor_tensor(rs[:, t0:t1], rs[:, t0:t1], half[:, t0:t1], ALU.pow), a, k_half)
            d = [DV.do(lambda e, t=t: e.tensor_scalar(X[:, b, t, :], X[:, b, t, :], mv[:, t, 0:1], rs[:, t:t + 1],
                                                      ALU.subtract, ALU.mult), a) for t in tiles]
            ln_free[:] = [d[-1]]
            x_tok[b] = d[-1]
            for t in tiles:
                x_prev[b, t // 2] = d[-1]
            return d[-1]

        def transpose_x(b):
            pieces = []
            toks = []

            def piece(kt, c):
                bk, ready, i = take()

                def mms(e):
                    for n in range(4):
                        last = e.transpose(bk[:, n * 128:n * 128 + 128],
                                           X[:, b, 4 * c + n, kt * 128:kt * 128 + 128], idF[:, :])
                    return last
                p = PE.do(mms, x_tok[b], ld_cst, ready)
                h = XH[:, kt, c * 512:c * 512 + 512]
                l = XL[:, kt, c * 512:c * 512 + 512]
                a = AC.do(lambda e: e.activation(h, bk[:, :], ACT.Copy), p, xh_free[0])
                d = DV.do(lambda e: e.tensor_tensor(l, bk[:, :], h.bitcast(F), ALU.subtract), a, xh_free[0])
                free(i, d)
                toks.append(a)
                toks.append(d)
                if len(toks) == 8:
                    xh_tok[0] = list(toks)
            for kt in range(2):
                for c in range(2):
                    pieces.append(lambda kt=kt, c=c: piece(kt, c))
            return pieces

        ctx_tok = [None]

        for b in range(NB):
            d = [DV.do(lambda e, t=t, b=b: e.tensor_tensor(X[:, b, t, :], X[:, b, t, :], boS, ALU.add),
                       ld_x[b], ld_bo) for t in range(NT)]
            x_tok[b] = d[-1]

        def load_ctx():
            z = PO.do(lambda e: e.memset(SH[1][:, :], 0.0), tmp_free[1])
            cv_ = SH[1][:, 0:NB * 2 * LP].rearrange("p (b k n) -> p b k n", b=NB, k=2)
            for b in range(NB):
                for k in range(2):
                    t = load("ctx", cv_[:, b, k, 0:L], cT[b, k * 128:k * 128 + 128, :], z)
            sf = [t2 for k2_, ts in set_free.items() if k2_[2] == 0 for t2 in ts]
            a = PO.do(lambda e: e.tensor_copy(CH, cv_), t, z, sf)
            d = PO.do(lambda e: e.tensor_tensor(CL, cv_, CH.bitcast(F), ALU.subtract), a, sf)
            tmp_free[1] = [tmp_free[1], d]
            ctx_tok[0] = d
            kx = REG[:, 2048:2048 + 12 * LP].bitcast(F).rearrange("p (b q k n) -> p b q k n", b=3, q=2, k=2)
            w = d
            for par in range(2):
                aug = 64 * (1 - par)
                w = PO.do(lambda e, a=kx[aug:aug + 64, :, par, 1, :]: e.memset(a, 0.0), w, sf)
                w = PO.do(lambda e, a=kx[aug:aug + 2, :, par, 1, :]: e.memset(a, 1.0), w)
            PO.wait(w)
            k_aug["x"] = w

        def after(u):
            return units[uidx[u] + 1] if uidx[u] + 1 < 4 else None

        def spread(slots, fs, a, b):
            for k, f in enumerate(fs):
                slots[a + k * (b - a) // len(fs)].append(f)

        def all_of(*lists):
            for fs in lists:
                for f in (fs if isinstance(fs, (list, tuple)) else [fs]):
                    f()

        st0, ps, ls = prep(units[0], 0)
        mx, least, turn, put = max_self(units[0], 0)
        all_of(st0, ps[0:2], ls[0:1], ps[2:3], ls[1:2], ps[3:4], ls[2:4], *vgroup(units[0], 0))
        all_of(mx, least, turn, put)

        pend = []

        def drain(n):
            while len(pend) > n:
                pv(*pend.pop(0))

        nprep = prep(units[0], 1)
        nprep[0]()
        carried = []
        for u in units[:2]:
            b = u[1]
            for h in range(NH):
                pair, par = h // 2, h % 2
                slots = [[] for _ in range(12)]
                prev = (u, pair - 1) if pair else (units[0], NP - 1) if u == units[1] else None
                nxt = (u, h + 1) if h + 1 < NH else (units[1], 0) if u == units[0] else None
                if nxt:
                    mx, least, turn, put = max_self(*nxt)
                else:
                    mx, least, turn, put = max_cross(units[2], 0)
                spread(slots, mx, 0, 8)
                slots[8].append(least)
                slots[9].append(turn)
                slots[10].append(put)
                if par == 0:
                    if prev:
                        weights, denoms, n0, n1, *carried = outproj(*prev)
                        slots[2].append(denoms)
                        slots[8].append(weights)
                        slots[3].append(n0)
                        slots[5].append(n1)
                    if pair + 1 == NP and u == units[0]:
                        slots[0].append(lambda: load_xT(1))
                    elif pair + 1 == NP:
                        slots[0].append(load_ctx)
                        slots[0].append(lambda: (load_w("wq1", 0, cq), load_w("wk1", 1, ck), load_w("wv1", 2, cv)))
                        spread(slots, transpose_x(0), 0, 3)
                        nprep = prep(units[2], 0)
                        slots[3].append(nprep[0])
                    _, ps, ls = nprep
                    a = 1 if pair + 1 < NP else 3
                    for n, f in enumerate(ps):
                        slots[a + (3 * n) // 2].append(f)
                    for n, f in enumerate(ls):
                        slots[a + 2 + (3 * n) // 2].append(f)
                    vg = None
                    if pair % 2:
                        if pair + 1 < NP:
                            vg = vgroup(u, pair // 2 + 1)
                        elif u == units[0]:
                            vg = vgroup(units[1], 0)
                    if vg:
                        slots[11].append(vg[0])
                else:
                    spread(slots, carried, 2, 9)
                    if prev and pair == 0:
                        slots[10].append(lambda: norm(0))
                    if vg:
                        spread(slots, vg[1], 1, 9)
                    elif pair + 1 == NP:
                        for g in range(4):
                            q = vgroup(units[2], g)
                            slots[9].append(q[0])
                            slots[9].extend(q[1])
                    nu = (u, pair + 2) if pair + 2 < NP else (units[uidx[u] + 1], 0)
                    if pair + 2 == NP:
                        nu = (units[1], 0) if u == units[0] else None
                    elif pair + 1 == NP:
                        nu = (units[1], 1) if u == units[0] else (units[2], 1)
                    if nu:
                        nprep = prep(*nu)
                        slots[11].append(nprep[0])
                n = 0
                for c in range(2):
                    for kt in range(4 * (c + 1)):
                        pend.append(scores(u, h, c, kt))
                        drain(2)
                        for f in slots[n]:
                            f()
                        n += 1

        drain(0)
        p_zero += [DV.do(lambda e, i=i: e.memset(PT[i][64:128, :], 0.0), P_free[i]) for i in range(3)]

        pairs = [(u, p) for u in units[2:] for p in range(NP)]
        all_of(nprep[1], nprep[2])
        nprep = prep(*pairs[2])
        nprep[0]()
        for n, (u, pair) in enumerate(pairs):
            weights, denoms, n0, n1, *ops = outproj(*pairs[n - 1]) if n else outproj(units[1], NP - 1)
            mx, least, turn, put = (max_cross(*pairs[n + 1]) if n + 1 < len(pairs)
                                    else ([], lambda: None, lambda: None, lambda: None))
            ps, ls = nprep[1:] if nprep else ([], [])
            weights()
            if n == 0:
                load_w("wo1", 3, co)
            pend.append(scores(u, 2 * pair, 0, 0))
            all_of(mx[0:2], denoms)
            pend.append(scores(u, 2 * pair, 1, 0))
            all_of(mx[2:4], ps[0:1])
            drain(1)
            pend.append(scores(u, 2 * pair + 1, 0, 0))
            all_of(ps[1:2], ls[0:1])
            drain(1)
            pend.append(scores(u, 2 * pair + 1, 1, 0))
            all_of(turn, n0, put, ls[1:2])
            drain(1)
            all_of(n1, ps[2:3])
            drain(0)
            all_of(ops[0:2], ls[2:3])
            if n == 6:
                all_of(ops[2:])
                ops = []
                for g in range(4):
                    all_of(*vgroup(units[3], g))
            if n + 3 < len(pairs):
                if n == 5:
                    all_of(transpose_x(1))
                nprep = prep(*pairs[n + 3])
                nprep[0]()
            else:
                nprep = None
            all_of(ops[2:])
            if n == 0:
                norm(1)
            if n == 8:
                norm(0)

        ff_ready = [t for ts in set_free.values() for t in ts]
        tW1 = load("W1", Wraw[0][:, :], W1, raw_free[0])
        tW2 = load("W2", Wraw[2][:, :], W2, raw_free[2])
        ld_wr = load("wr", wrS, wr, rope_last)
        tb2 = load("b2", b2S, b2, rope_last)
        WH = [REG[:, 1024 * i:1024 * i + 2048] for i in (4, 12, 6, 14)]
        a1 = PO.do(lambda e: e.tensor_copy(WH[0], Wraw[0][:, :]), tW1, ff_ready)
        l1 = PO.do(lambda e: e.tensor_tensor(WH[1], Wraw[0][:, :], WH[0].bitcast(F), ALU.subtract), a1)
        a2 = PO.do(lambda e: e.tensor_copy(WH[2], Wraw[2][:, :]), tW2, ff_ready)
        l2 = PO.do(lambda e: e.tensor_tensor(WH[3], Wraw[2][:, :], WH[2].bitcast(F), ALU.subtract), a2)
        w1h, w1l = (w.rearrange("p (k n) -> p k n", k=2) for w in WH[0:2])
        w2h, w2l = (w.rearrange("p (k n) -> p k n", k=8) for w in WH[2:4])
        NC4 = 256
        HH = [REG[:, 1024 * i:1024 * i + 2048].rearrange("p (k n) -> p k n", k=8) for i in (10, 0)]
        HL = [REG[:, 1024 * i:1024 * i + 2048].rearrange("p (k n) -> p k n", k=8) for i in (8, 2)]
        h_free = [None] * 2
        hf_free = [None] * 2
        blend_tok = [P_free, None]
        router = {}

        def route(b):
            dd = []
            for t in range(NT):
                tmp = NU[0][:, 0:C]
                a = DV.do(lambda e, t=t: e.tensor_tensor(tmp, X[:, b, t, :], wrS, ALU.mult),
                          x_tok[b], ld_wr, nu_free, dd[-1] if dd else None)
                dd.append(DV.do(lambda e, t=t: e.tensor_reduce(wl[:, t:t + 1], tmp, AX.X, ALU.add), a,
                                router.get("wl")))
            a = DV.do(lambda e: e.tensor_scalar(wl[:, :], wl[:, :], brS[:, 0:1], None, ALU.add), dd)
            cc = []

            def count(j):
                bk, ready, i = take()
                for n in range(4):
                    t = 4 * j + n
                    wb = NU[0][:, 256 + 128 * (n % 2):384 + 128 * (n % 2)]
                    c = DV.do(lambda e, t=t, wb=wb: e.tensor_copy(wb, wl[:, t:t + 1].to_broadcast([128, 128])),
                              a, router.get(n % 2))
                    ps = PE.do(lambda e, n=n, wb=wb: e.transpose(bk[:, n * 128:n * 128 + 128], wb, idF[:, :]),
                               c, ready)
                    router[n % 2] = ps
                for t in range(NT):
                    k = DV.do(lambda e, t=t: e.tensor_scalar(
                        NU[0][:, 512:1024], bk[:, :], wl[:, t:t + 1], None, ALU.is_ge, ALU.add,
                        accum_out=cnt[:, t, j:j + 1]), ps, router.get("sel"), cc[-1] if cc else None)
                    cc.append(k)
                free(i, k)
            count(0)
            count(1)
            a = DV.do(lambda e: e.tensor_tensor(cnt[:, :, 0], cnt[:, :, 0], cnt[:, :, 1], ALU.add), cc)
            router["wl"] = a
            return DV.do(lambda e: e.tensor_scalar(sel[:, :], cnt[:, :, 0], TOP - 0.5, None, ALU.is_lt),
                         a, router.get("blend"))

        def hidden(b, q):
            i2 = (b * 4 + q) % 2
            qs = slice(q * NC4, q * NC4 + NC4)
            toks = []

            def tile(m):
                bk, ready, i = take()

                def mms(e):
                    for n in range(2):
                        hs = slice((2 * m + n) * 128, (2 * m + n) * 128 + 128)
                        terms = []
                        for k in range(2):
                            terms += [(w1h[:, k, hs], XH[:, k, qs]), (w1h[:, k, hs], XL[:, k, qs]),
                                      (w1l[:, k, hs], XH[:, k, qs])]
                        last = mm3(e, bk[:, n * 256:n * 256 + 256], terms)
                    return last
                p = PE.do(mms, xh_tok[0], l1, ready)
                xh_free[0] = p
                j = m % 2
                for n in range(2):
                    g = AC.do(lambda e, n=n, j=j: e.activation(
                        T1[j][:, n * 256:n * 256 + 256], bk[:, n * 256:n * 256 + 256], ACT.Gelu,
                        bias=b1S[:, 2 * m + n:2 * m + n + 1], scale=1.0), p, ld_sm, tmp_free[j])
                free(i, g)
                hh = HH[i2][:, 2 * m:2 * m + 2, :].rearrange("p k n -> p (k n)")
                hl = HL[i2][:, 2 * m:2 * m + 2, :].rearrange("p k n -> p (k n)")
                a = DV.do(lambda e, j=j, hh=hh: e.tensor_copy(hh, T1[j][:, :]), g, h_free[i2], ff_ready)
                d = DV.do(lambda e, j=j, hh=hh, hl=hl: e.tensor_tensor(hl, T1[j][:, :], hh.bitcast(F),
                                                                       ALU.subtract), a)
                tmp_free[j] = d
                toks.extend([a, d])
            for m in range(4):
                tile(m)
            return toks

        def finish(b, q, toks, sl_tok):
            i2 = (b * 4 + q) % 2
            bk, ready, i = take()

            def mms(e):
                for n in range(2):
                    ts = slice(n * 128, n * 128 + 128)
                    terms = []
                    for k in range(8):
                        terms += [(HH[i2][:, k, ts], w2h[:, k, :]), (HH[i2][:, k, ts], w2l[:, k, :]),
                                  (HL[i2][:, k, ts], w2h[:, k, :])]
                    last = mm3(e, bk[:, n * 256:n * 256 + 256], terms)
                return last
            p = PE.do(mms, toks, l2, ready)
            h_free[i2] = p
            for n in range(2):
                t = 2 * q + n
                xs = X[:, b, t, :]
                y = PT[n][:, 0:256]
                a = DV.do(lambda e, n=n, y=y: e.tensor_tensor(y, bk[:, n * 256:n * 256 + 256], b2S, ALU.add),
                          p, tb2, P_free[n], router.get(("y", n)))
                z = DV.do(lambda e, t=t, xs=xs: e.tensor_scalar(xs, xs, nsel[:, t:t + 1], None, ALU.mult),
                          sl_tok, x_tok[b])
                d = DV.do(lambda e, t=t, xs=xs, y=y: e.scalar_tensor_tensor(xs, y, sel[:, t:t + 1], xs,
                                                                            ALU.mult, ALU.add), a, z)
                router["y", n] = d
                x_prev[b, t // 2] = d
            free(i, a)
            router["blend"] = d

        nsel = sb("nsel", [128, NT])
        outs = []
        for b in range(NB):
            for f in transpose_x(b):
                f()
            if b == 0:
                last = outproj(*pairs[-1])
                last[0]()
                last[1]()
            tk = hidden(b, 0)
            if b == 0:
                for f in last[2:]:
                    f()
                norm(1)
            s = route(b)
            sl_tok = [s, DV.do(lambda e: e.tensor_scalar(nsel[:, :], sel[:, :], -1.0, 2.0, ALU.mult, ALU.add),
                               s, router.get("blend"))]
            for q in range(4):
                nx = hidden(b, q + 1) if q < 3 else None
                finish(b, q, tk, sl_tok)
                d = norm(b, [2 * q, 2 * q + 1])
                outs.append(load("out", out[b, q * 256:q * 256 + 256, :].rearrange("(n p) c -> p n c", p=128),
                                 X[:, b, 2 * q:2 * q + 2, :], d))
                tk = nx
        SP.wait(outs[-1])

        @block.sync
        def _(e):
            SP.run(e)

        @block.scalar
        def _(e):
            AC.run(e)

        @block.vector
        def _(e):
            DV.run(e)

        @block.gpsimd
        def _(e):
            PO.run(e)

        @block.tensor
        def _(e):
            PE.run(e)


def kernel(**inputs):
    import numpy as np
    import concourse.bacc as _bacc
    from concourse import mybir as _mybir
    from concourse.bass_utils import run_bass_kernel_spmd as _run

    g = {k: np.asarray(v) for k, v in inputs.items()}

    def rows(w, k):
        return w.reshape(k, 128, -1).transpose(1, 0, 2).reshape(128, -1)

    inv = (1.0 / np.float32(10000.0) ** (np.arange(0, D, 2, dtype=np.float32) / np.float32(D))).astype(np.float32)
    ang = np.arange(T, dtype=np.float32)[:, None] * inv[None, :]
    sn, cs = np.sin(ang).astype(np.float32), np.cos(ang).astype(np.float32)
    cosT = np.tile(np.repeat(cs.T, 2, axis=0), (2, 1))
    sinT = np.repeat(sn.T, 2, axis=0)
    sinT[0::2] = -sinT[0::2]
    sinT = np.tile(sinT, (2, 1))
    i = np.arange(128)
    feed = {
        "xT": g["x"].transpose(0, 2, 1), "x": g["x"], "cT": g["ctx_1024"].transpose(0, 2, 1),
        "Wq": rows(g["L0_attn_Wq"], 2), "Wk": rows(g["L0_attn_Wk"], 2), "Wv": rows(g["L0_attn_Wv"], 2),
        "Wo": rows(g["L0_attn_Wo"], 8), "bo": np.tile(g["L0_attn_bo"][None], (128, 1)),
        "cq": rows(g["L0_xattn_w_q"], 2), "ck": rows(g["L0_xattn_w_k"], 2), "cv": rows(g["L0_xattn_w_v"], 2),
        "co": rows(g["L0_xattn_w_o"], 8), "wr": np.tile(g["L0_ffn_w_r"].reshape(1, -1), (128, 1)),
        "br": np.tile(g["L0_ffn_b_r"].reshape(1, 1), (128, 1)),
        "W1": rows(g["L0_ffn_W1"], 2), "b1": g["L0_ffn_b1"].reshape(8, 128).T,
        "W2": rows(g["L0_ffn_W2"], 8), "b2": np.tile(g["L0_ffn_b2"][None], (128, 1)),
        "cosT": cosT, "sinT": sinT, "identd": np.eye(128, dtype=np.float32),
        "maskqk": np.where(i[None, :] > i[:, None], np.float32(NEG), np.float32(0)),
    }
    nc = _bacc.Bacc("TRN2", target_bir_lowering=False, num_devices=1)
    arrays, args = {}, []
    for name, a in feed.items():
        a = np.ascontiguousarray(a)
        arrays["in_" + name] = a
        args.append(nc.dram_tensor("in_" + name, a.shape, _mybir.dt.from_np(a.dtype), kind="ExternalInput").ap())
    args.append(nc.dram_tensor("out_0", (NB, T, C), _mybir.dt.float32, kind="ExternalOutput").ap())
    build(nc, *args)
    r = _run(nc, [arrays], core_ids=[0])
    return r.results[0]["out_0"]
```

```python
import concourse.bass as bass
from concourse import mybir
from contextlib import ExitStack

F = mybir.dt.float32
R = mybir.dt.float32r
BF = mybir.dt.bfloat16
ALU = mybir.AluOpType
ACT = mybir.ActivationFunctionType
AX = mybir.AxisListType

NB, T, C, NH, D = 2, 1024, 256, 16, 64
L = 77
LP = 78
NP = NH // 2
NT = T // 128
TOP = 512
NEG = -1.0e30
EPS = 1e-5
SWAP = [i ^ 1 for i in range(32)]


EVERY = {
    "m0": 1.09, "m1": 1.63, "m6": 1.81, "m4": 1.95, "m3": 2.04, "m2": 2.51, "m5": 2.77, "m8": 3.06,
    "m7": 3.17, "m9": 3.83, "turn0": 3.88, "put0": 4.51, "m10": 4.74, "m11": 5.13, "least": 7.47,
    "turn1": 8.01, "put1": 9.57}
EVEN = {
    "p0": 0.73, "l0": 2.79, "denoms": 2.86, "p1": 3.48, "n0": 4.31, "weights": 4.32, "p2": 4.7, "l1": 4.8,
    "p3": 5.49, "vsplit": 7.39, "n1": 7.68, "l2": 8.7, "l3": 9.25}
ODD = {
    "v0": 0.25, "o0": 0.69, "o1": 0.87, "v1": 1.39, "o3": 2.12, "v2": 4.65, "o2": 6.7, "v3": 7.94,
    "psplit": 10.03}
CROSS = {
    "o2": 0.0, "denoms": 0.07, "t0": 0.12, "o3": 0.44, "m0": 0.68, "weights": 0.98, "w0": 1.01, "norm": 1.06,
    "m1": 1.08, "t1": 1.09, "w2": 1.3, "pv0": 1.38, "n0": 1.46, "n1": 1.62, "p0": 1.72, "m2": 1.92,
    "r0": 2.0, "w1": 2.08, "l0": 2.12, "p1": 2.2, "turn0": 2.3, "t2": 2.3, "m3": 2.5, "put0": 2.6,
    "pv1": 2.73, "r1": 2.75, "o0": 2.83, "pv2": 2.86, "l1": 3.02, "p2": 3.34, "r2": 3.35, "turn1": 3.41,
    "l2": 3.68, "w3": 3.75, "pv3": 3.9, "t3": 3.93, "o1": 3.94, "put1": 4.35}

LAST = {
    "x0": 0.29, "x1": 0.8, "m0": 1.0, "x2": 2.1, "x3": 2.2, "m1": 2.9, "psplit": 3.0, "p0": 3.1,
    "turn0": 4.0, "p1": 4.1, "m2": 4.7, "l1": 5.08, "l0": 5.2, "m3": 6.0, "p2": 6.53, "p3": 7.1,
    "put0": 7.11, "v": 7.25, "turn1": 8.9, "l2": 9.09, "l3": 9.7, "put1": 9.72, "norm": 9.9}


class Engine:

    def __init__(self, sem):
        self.sem, self.count, self.queue, self.seen = sem, 0, [], {}

    def wait(self, *tokens):
        for tok in tokens:
            if tok is None:
                continue
            if isinstance(tok, list):
                self.wait(*tok)
                continue
            sem, value = tok
            if self.seen.get(sem, 0) < value:
                self.seen[sem] = value
                self.queue.append(lambda e, s=sem, v=value: e.wait_ge(s, v))

    def do(self, fn, *waits):
        self.wait(*waits)
        self.count += 1
        self.queue.append(lambda e: fn(e).then_inc(self.sem, 1))
        return (self.sem, self.count)

    def run(self, e):
        for f in self.queue:
            f(e)


def build(nc, xT, x, cT, Wq, Wk, Wv, Wo, bo, cq, ck, cv, co, wr, br, W1, b1, W2, b2, cosT, sinT,
          identd, maskqk, out):
    ctx = ExitStack()
    with ctx:
        def sb(name, shape, dt=F):
            return ctx.enter_context(nc.sbuf_tensor(name, shape, dt))

        def sem(name):
            return ctx.enter_context(nc.semaphore(name))

        PE, AC, DV, PO, SP = (Engine(sem(n)) for n in ("s_pe", "s_act", "s_dve", "s_pool", "s_sp"))
        dma_sems = {}

        def load(name, dst, src, *waits):
            SP.wait(*waits)
            if name not in dma_sems:
                dma_sems[name] = [sem("d_" + name), 0]
            d = dma_sems[name]
            d[1] += 16
            SP.queue.append(lambda e: e.dma_start(dst, src).then_inc(d[0], 16))
            return (d[0], d[1])

        Wraw = [sb(f"Wraw{i}", [128, 2048]) for i in range(4)]
        SLH = [sb(f"SLH{i}", [128, 512], R) for i in range(2)]
        SLL = [sb(f"SLL{i}", [128, 512], R) for i in range(2)]
        REG = sb("REG", [128, 16384], R)
        XH = sb("XH", [128, 2, T], R)
        XL = sb("XL", [128, 2, T], R)
        VV = [sb(f"VV{i}", [128, NT, 384]) for i in range(2)]
        OH = sb("OH", [128, T], R)
        OL = sb("OL", [128, T], R)
        NU = [sb(f"NU{i}", [128, T]) for i in range(2)]
        RBC = [sb(f"RBC{i}", [128, 512]) for i in range(2)]
        DR = sb("DR", [128, 512])
        RCP = [sb(f"RCP{i}", [128, 4, 4]) for i in range(2)]
        X = sb("X", [128, NB, NT, C])
        PT = [sb(f"PT{i}", [128, 512]) for i in range(3)]
        cosS = sb("cosS", [128, T])
        sinS = sb("sinS", [128, T])
        T1 = [sb(f"T1{i}", [128, 512]) for i in range(2)]
        SH = [sb(f"SH{i}", [128, 512]) for i in range(2)]
        NM = [sb(f"NM{i}", [128, 16]) for i in range(2)]
        MH = [sb(f"MH{i}", [16, 128], R) for i in range(2)]
        ML = [sb(f"ML{i}", [16, 128], R) for i in range(2)]
        idF = sb("idF", [128, 128])
        idB = sb("idB", [128, 128], BF)
        mQK = sb("mQK", [128, 128], BF)
        boS = NU[1][:, 0:C]
        b2S = cosS[:, C:2 * C]
        wrS = cosS[:, 0:C]
        b1S = sb("b1S", [128, NT])
        brS = sb("brS", [128, 1])
        st = sb("st", [128, NT, 6])
        mv = sb("mv", [128, NT, 2])
        rs = sb("rs", [128, NT])
        half = sb("half", [128, NT])
        wlS, selS, nselS = ([sinS[:, 64 * b + o:64 * b + o + NT] for b in range(NB)] for o in (0, 8, 16))
        cntS = [sinS[:, 64 * b + 24:64 * b + 40].rearrange("p (t j) -> p t j", j=2) for b in range(NB)]

        bank = [ctx.enter_context(nc.psum_tensor(f"bank{i}", [128, 512], F)) for i in range(8)]
        ST, OB, RB = bank[0:2], bank[2:4], bank[4:8]
        block = ctx.enter_context(nc.Block())

        def setview(kind, par, buf):
            o = ((par * 2 + buf) * 4 + kind) * 1024
            return REG[:, o:o + 1024]

        CH, CL = (REG[:, 3072 + 512 * n:3072 + 512 * n + NB * 2 * LP].rearrange(
            "p (b k n) -> p b k n", b=NB, k=2) for n in range(2))
        XQ = [0, 4, 6]

        def view(u, pair, par, kind):
            if u[0] == "self":
                return setview(kind, par, (uidx[u] * NP + pair) % 2)
            bf = ((uidx[u] - 2) * NP + pair) % 3
            if kind < 2:
                o = (8 * par + XQ[bf] + kind) * 1024
                return REG[:, o:o + 1024]
            o = 2048 + ((bf * 2 + par) * 2 + kind - 2) * LP
            return REG[:, o:o + LP]

        def setkey(u, pair, par):
            return (par, (uidx[u] % 2 * NP + pair) % (2 if u[0] == "self" else 3))

        units = [("self", 0), ("self", 1), ("cross", 0), ("cross", 1)]
        uidx = {u: n for n, u in enumerate(units)}

        ring = [(n, None) for n in range(4)]

        def take():
            i, tok = ring.pop(0)
            return RB[i], tok, i

        def free(i, tok):
            ring.append((i, tok))

        raw_free = [None] * 4
        raw_tok = {}

        def load_w(key, slot, ap):
            raw_tok[key] = load(key, Wraw[slot][:, :], ap, raw_free[slot])

        tmp_free = [None] * 4

        xh_free = [None]
        xh_tok = [None]
        tn = [0]
        set_free = {}

        def load_xT(b, v):
            raw = VV[v][:, :, :].rearrange("p t n -> p (t n)")
            toks, pieces = [[], []], []

            def piece(c, kt):
                cs = slice(c * 512, c * 512 + 512)
                raw_, t = raw[:, 1024 * kt + 512 * c:1024 * kt + 512 * c + 512], ld_xT[b, kt, c]
                h, l = XH[:, kt, cs], XL[:, kt, cs]
                a = AC.do(lambda e: e.activation(h, raw_, ACT.Copy), t, xh_free[0])
                d = DV.do(lambda e: e.tensor_tensor(l, raw_, h.bitcast(F), ALU.subtract), a, t, xh_free[0])
                raw_read.extend([a, d])
                toks[c] += [a, d]
                xh_tok[0] = toks
            return [lambda c=c, kt=kt: piece(c, kt) for c in range(2) for kt in range(2)]

        def fetch_xT(b, v, c, kt, *waits):
            ld_xT[b, kt, c] = load(f"x{b}{kt}{c}", VV[v][:, :, :].rearrange("p t n -> p (t n)")[
                :, 1024 * kt + 512 * c:1024 * kt + 512 * c + 512],
                xT[b, kt * 128:kt * 128 + 128, c * 512:c * 512 + 512], *waits)

        def part(ap, k0, n):
            return ap.rearrange("p (k n) -> p k n", k=2)[:, :, k0:k0 + n]

        ld_xT = {}
        raw_read = []
        for c in range(2):
            cs = slice(c * 512, c * 512 + 512)
            if c == 0:
                raw_tok["wk0", 0] = load("wk00", part(Wraw[1][:, :], 0, 128), part(Wk, 0, 128))
                raw_tok["wq0", 0] = load("wq00", part(Wraw[0][:, :], 0, 128), part(Wq, 0, 128))
            for kt in range(2):
                fetch_xT(0, 1, c, kt)
            if c == 0:
                ld_cst = load("cst", idF[:, :], identd)
                mtmp = load("msk", T1[0][:, 0:128], maskqk)
            load(f"rope{c}", cosS[:, cs], cosT[:, cs])
            ld_rope = load(f"rope{c}", sinS[:, cs], sinT[:, cs])
            ld_ropes = [ld_rope] if c == 0 else [ld_ropes[0], ld_rope]
            if c == 0:
                raw_tok["wv0", 0] = load("wv00", part(Wraw[2][:, :], 0, 256), part(Wv, 0, 256))
        raw_tok["wq0"] = load("wq0", part(Wraw[0][:, :], 128, 896), part(Wq, 128, 896))
        raw_tok["wk0"] = load("wk0", part(Wraw[1][:, :], 128, 896), part(Wk, 128, 896))
        raw_tok["wv0"] = load("wv0", part(Wraw[2][:, :], 256, 768), part(Wv, 256, 768))

        k_idb = AC.do(lambda e: e.activation(idB[:, :], idF[:, :], ACT.Copy), ld_cst)
        for f in load_xT(0, 1):
            f()
        k_mqk = AC.do(lambda e: e.activation(mQK[:, :], T1[0][:, 0:128], ACT.Copy), mtmp)
        k_cst = [k_idb, k_mqk]
        tmp_free[0] = k_mqk

        load_w("wo0", 3, Wo)
        ld_x = [load(f"x{b}", X[:, b, :, :], x[b].rearrange("(n p) c -> p n c", p=128)) for b in range(NB)]
        ld_bo = load("bo", boS, bo)
        ld_sm = load("sm", b1S[:, :], b1)
        ld_sm = load("sm", brS[:, :], br)

        def ones(n, *waits):
            v = VV[n][:, :, :].rearrange("p t (a s d) -> p t a s d", a=2, s=3)[:, :, :, 1, :]
            return PO.do(lambda e: e.memset(v, 1.0), *waits)
        k_ones = [ones(0), None]
        k_half = PO.do(lambda e: e.memset(half[:, :], -0.5))
        k_aug = {}

        sl = {"n": 0, "free": [None] * 2}
        left_of = [0, 0]

        def split(parts, uses):
            i = sl["n"] % 2
            assert left_of[i] == 0
            left_of[i] = uses
            sl["n"] += 1
            o, toks = 0, []
            for raw, slot, tok in parts:
                shp = raw.shape[1:]
                n = 1
                for s in shp:
                    n *= s
                h, l = SLH[i][:, o:o + n], SLL[i][:, o:o + n]
                if len(shp) == 2:
                    h = h.rearrange("p (a b) -> p a b", a=shp[0])
                    l = l.rearrange("p (a b) -> p a b", a=shp[0])
                a = AC.do(lambda e, h=h, r=raw: e.activation(h, r, ACT.Copy), tok, sl["free"][i])
                d = PO.do(lambda e, h=h, l=l, r=raw: e.tensor_tensor(l, r, h.bitcast(F), ALU.subtract),
                          a, sl["free"][i])
                raw_free[slot] = d
                toks.append(d)
                o += n
            return i, toks[-1]

        def wview(slot):
            return Wraw[slot][:, :].rearrange("p (k n) -> p k n", k=2)

        def woview(slot):
            return Wraw[slot][:, :].rearrange("p (k n) -> p k n", k=8)

        def mm3(e, o, terms):
            for n, (a, b) in enumerate(terms):
                last = e.matmul(o, a, b, start=n == 0, stop=n == len(terms) - 1)
            return last

        rope_last = []
        set_tok = {}
        P_free = [None] * 3

        def x_wait(u, pair):
            if u == units[2] and pair < 3:
                return [t for k, ts in set_free.items() if k[0] == "self" and (pair or k[2] == 0) for t in ts]
            return []

        def prep(u, pair):
            kind, b = u
            first_pair = u == units[0] and pair == 0
            key = "0" if kind == "self" else "1"
            pc = slice(pair * 128, pair * 128 + 128)
            pieces = []
            box = {}

            def start():
                box["s"], box["t"] = split([(wview(0)[:, :, pc], 0, raw_tok["wq0", 0] if first_pair else raw_tok["wq" + key]),
                                            (wview(1)[:, :, pc], 1, raw_tok["wk0", 0] if first_pair else raw_tok["wk" + key])], 4 if kind == "self" else 3)
                for par in range(2):
                    set_tok[u, pair, par] = [k_aug["x"] if kind == "cross" else k_aug.get(par)]

            def proj(which, c):
                s = box["s"]
                wh = SLH[s][:, which * 256:which * 256 + 256].rearrange("p (k n) -> p k n", k=2)
                wlo = SLL[s][:, which * 256:which * 256 + 256].rearrange("p (k n) -> p k n", k=2)
                if kind == "self" or which == 0:
                    w = 512
                    xh = [XH[:, k, c * 512:c * 512 + 512] for k in range(2)]
                    xl = [XL[:, k, c * 512:c * 512 + 512] for k in range(2)]
                    dep = xh_tok[0][c]
                else:
                    w = LP
                    xh = [CH[:, b, k, :] for k in range(2)]
                    xl = [CL[:, b, k, :] for k in range(2)]
                    dep = ctx_tok[0]
                bk, ready, i = take()
                terms = []
                for k in range(2):
                    terms += [(wh[:, k, :], xh[k]), (wh[:, k, :], xl[k]), (wlo[:, k, :], xh[k])]
                p = PE.do(lambda e: mm3(e, bk[:, 0:w], terms), box["t"], dep, ready)
                sl["free"][s] = p
                left_of[s] -= 1
                if kind == "self" or which == 0:
                    xh_free[0] = p
                cs = slice(c * 512, c * 512 + w)
                j = tn[0] % 2
                if kind == "self":
                    tn[0] += 1
                    tt, sh = T1[j][:, :], SH[j][:, :]
                    if first_pair and c == 1:
                        j, tt, sh = 2 + which, NU[0][:, which * 512:which * 512 + 512], PT[which][:, :]
                    EG = DV if first_pair and (which == 1 or c == 0) else PO
                    a = DV.do(lambda e: e.tensor_tensor(tt, bk[:, :], cosS[:, cs], ALU.mult),
                              p, ld_ropes[c], tmp_free[j])
                    d = DV.do(lambda e: e.stream_shuffle(sh, bk[:, :], SWAP))
                    free(i, d)
                    rope_last[:] = [a]
                    g = EG.do(lambda e: e.tensor_tensor(sh, sh, sinS[:, cs], ALU.mult), d, ld_ropes[c])
                    g = EG.do(lambda e: e.tensor_tensor(tt, tt, sh, ALU.add), g, a)
                    src, dep2 = tt, g
                else:
                    src, dep2 = bk[:, 0:w], p
                def parts():
                    store(which, w, cs, src, dep2, i, j)
                return parts

            def store(which, w, cs, src, dep2, i, j):
                hi = []
                frees = [set_free.get((u[0], *setkey(u, pair, par)), []) + x_wait(u, pair) for par in range(2)]
                for par in range(2):
                    base = 64 * par
                    t = view(u, pair, par, 0 if which == 0 else 2)[base:base + 64, cs]
                    hi.append(AC.do(lambda e, t=t, s=src[base:base + 64, :]: e.activation(t, s, ACT.Copy),
                                    dep2, frees[par]))
                lo = []
                for par in range(2):
                    base, aug = 64 * par, 64 * (1 - par)
                    t = view(u, pair, par, 0 if which == 0 else 2)[base:base + 64, cs]
                    l = (view(u, pair, par, 0)[aug:aug + 64, cs] if which == 0
                         else view(u, pair, par, 3)[base:base + 64, cs])
                    on = PO if kind == "self" and which == 1 and not first_pair else DV
                    if on is PO and par:
                        PO.wait((PO.sem, PO.count))
                    lo.append(on.do(lambda e, t=t, l=l, s=src[base:base + 64, :]: e.tensor_tensor(
                        l, s, t.bitcast(F), ALU.subtract), hi, dep2, frees[par]))
                if kind == "self":
                    tmp_free[j] = lo
                    if on is PO:
                        PO.wait(lo[-1])
                else:
                    free(i, lo[-1])
                for par in range(2):
                    base, aug = 64 * par, 64 * (1 - par)
                    t = view(u, pair, par, 0 if which == 0 else 2)[base:base + 64, cs]
                    dup = (view(u, pair, par, 1)[base:base + 64, cs] if which == 0
                           else view(u, pair, par, 2)[aug:aug + 64, cs])
                    k = load(f"dup{which}{par}{cs.start // 512}", dup.bitcast(F), t.bitcast(F), hi[par], frees[par])
                    set_tok[u, pair, par] += [k, lo[par]]

            order = [(1, 0), (0, 0), (1, 1), (0, 1)] if kind == "self" else [(1, 0), (0, 0), (0, 1)]
            later = {}

            def first(n, w_, c_):
                later[n] = proj(w_, c_)
            return (start, [lambda n=n, w_=w_, c_=c_: first(n, w_, c_) for n, (w_, c_) in enumerate(order)],
                    [lambda n=n: later[n]() for n in range(len(order))])

        vv_free = [None] * 2
        vv_tok = {}

        def vgroup(u, g):
            kind, b = u
            v = (uidx[u] * 4 + g) % 2 if kind == "self" else uidx[u] % 2
            key = "0" if kind == "self" else "1"
            box = {}

            def start():
                box["s"], box["t"] = split([(wview(2)[:, :, g * 256:g * 256 + 256], 2,
                                             raw_tok["wv0", 0] if u == units[0] and g == 0 else raw_tok["wv" + key])], 4 if kind == "self" else 1)
                vv_tok[u, g] = [k_ones[v]]

            def piece(j):
                s = box["s"]
                wh = SLH[s][:, :].rearrange("p (k n) -> p k n", k=2)
                wlo = SLL[s][:, :].rearrange("p (k n) -> p k n", k=2)
                bk, ready, i = take()
                tiles = [2 * j, 2 * j + 1] if kind == "self" else [0]
                rows = 128 if kind == "self" else L

                def mms(e):
                    for n, t in enumerate(tiles):
                        if kind == "self":
                            xh = [XH[:, k, t * 128:t * 128 + 128] for k in range(2)]
                            xl = [XL[:, k, t * 128:t * 128 + 128] for k in range(2)]
                        else:
                            xh = [CH[:, b, k, 0:L] for k in range(2)]
                            xl = [CL[:, b, k, 0:L] for k in range(2)]
                        terms = []
                        for k in range(2):
                            terms += [(xh[k], wh[:, k, :]), (xh[k], wlo[:, k, :]), (xl[k], wh[:, k, :])]
                        last = mm3(e, bk[0:rows, n * 256:n * 256 + 256], terms)
                    return last
                p = PE.do(mms, box["t"], xh_tok[0][j // 2] if kind == "self" else ctx_tok[0], ready)
                sl["free"][s] = p
                left_of[s] -= 1
                if kind == "self":
                    xh_free[0] = p
                for n, t in enumerate(tiles):
                    dst = VV[v][0:rows, t if kind == "self" else g, :].rearrange("p (a s d) -> p a s d", a=2, s=3)[:, :, 0:3:2, :]
                    src = bk[0:rows, n * 256:n * 256 + 256].rearrange("p (a s d) -> p a s d", a=2, s=2)
                    k = AC.do(lambda e, dst=dst, src=src: e.activation(dst, src, ACT.Copy), p, vv_free[v])
                free(i, k)
                vv_tok[u, g].append(k)

            n = 4 if kind == "self" else 1

            return start, [lambda j=j: piece(j) for j in range(n)]

        rows_tok = {}
        nm_free = [None] * 2
        mh_free = [None] * 2

        def max_self(u, h):
            pair, par = h // 2, h % 2
            q1, k1 = view(u, pair, par, 0), view(u, pair, par, 2)
            m = h % 2
            toks = []

            def chunk(qt, kc):
                k0 = kc * 512
                w = min(512, (qt + 1) * 128 - k0)
                diag = (qt + 1) * 128 <= k0 + 512
                col = qt if kc == 0 else 4 + qt
                bk, ready, i = take()

                def mms(e):
                    last = e.matmul(bk[:, 0:w], q1[:, qt * 128:qt * 128 + 128], k1[:, k0:k0 + w],
                                    start=True, stop=not diag)
                    if diag:
                        last = e.matmul(bk[:, w - 128:w], idB[:, :], mQK[:, :], start=False, stop=True)
                    return last
                p = PE.do(mms, set_tok[u, pair, par], k_cst, ready)
                d = DV.do(lambda e: e.tensor_reduce(NM[m][:, col:col + 1], bk[:, 0:w], AX.X, ALU.max,
                                                    negate=True), p, nm_free[m])
                free(i, d)
                toks.append(d)

            box = {}

            def least():
                assert len(toks) == 12
                box[1] = DV.do(lambda e: e.tensor_tensor(NM[m][:, 4:8], NM[m][:, 4:8], NM[m][:, 8:12], ALU.min),
                               toks[4:])

            def turn(c):
                if c == 0:
                    assert len(toks) >= 4
                    box[0] = toks[0:4]
                box["f", c] = to_rows(u, m, c, 4 * c, 4, box[c], pair, par, c * 512)
            order = [(qt, kc) for qt in range(NT) for kc in range(qt // 4 + 1)]
            return ([lambda qt=qt, kc=kc: chunk(qt, kc) for qt, kc in order],
                    {"turn0": lambda: turn(0), "put0": lambda: box["f", 0](), "least": least,
                     "turn1": lambda: turn(1), "put1": lambda: box["f", 1]()})

        def to_rows(u, m, r, c0, n, dep, pair, par, q0):
            bk, ready, i = take()
            p = PE.do(lambda e: e.transpose(bk[0:n, 0:128], NM[m][:, c0:c0 + n], idF[:, :]), dep, ld_cst, ready)
            nm_free[m] = p

            def put():
                a = DV.do(lambda e: e.tensor_copy(MH[r][0:n, :], bk[0:n, 0:128]), p, mh_free[r])
                d = DV.do(lambda e: e.tensor_tensor(ML[r][0:n, :], bk[0:n, 0:128], MH[r][0:n, :].bitcast(F),
                                                    ALU.subtract), a, mh_free[r])
                free(i, d)
                mh_free[r] = []
                q2 = view(u, pair, par, 1)
                aug = 64 * (1 - par)
                for s, (src, dep2) in enumerate(((MH[r], a), (ML[r], d))):
                    t = load(f"rows{r}", q2[aug + s:aug + s + 1, q0:q0 + 128 * n].bitcast(F),
                             src[0:n, :].bitcast(F), dep2,
                             set_free.get((u[0], *setkey(u, pair, par)), []) + x_wait(u, pair))
                    mh_free[r].append(t)
                for c in range(q0 // 512, (q0 + 128 * n) // 512):
                    rows_tok[u, pair, par, c] = t
            return put

        def max_cross(u, pair):
            m = pair % 2
            toks = []

            def chunk(par, j):
                q1, k1 = view(u, pair, par, 0), view(u, pair, par, 2)
                bk, ready, i = take()

                def mms(e):
                    for n in range(4):
                        qt = 4 * j + n
                        last = e.matmul(bk[:, n * 128:n * 128 + LP], q1[:, qt * 128:qt * 128 + 128],
                                        k1[:, 0:LP], start=True, stop=True)
                    return last
                p = PE.do(mms, set_tok[u, pair, par], ready)
                c0 = 8 * par + 4 * j
                d = DV.do(lambda e: e.tensor_reduce(
                    NM[m][:, c0:c0 + 4], bk[:, :].rearrange("p (n k) -> p n k", n=4)[:, :, 0:L],
                    AX.X, ALU.max, negate=True), p, nm_free[m])
                free(i, d)
                toks.append(d)

            box = {}

            def turn(par):
                assert len(toks) >= 2 * par + 2
                box[par] = to_rows(u, m, par, 8 * par, 8, toks[2 * par:2 * par + 2], pair, par, 0)
            return ([lambda par=par, j=j: chunk(par, j) for par in range(2) for j in range(2)],
                    {"turn0": lambda: turn(0), "put0": lambda: box[0](),
                     "turn1": lambda: turn(1), "put1": lambda: box[1]()})

        st_free = [None] * 2
        o_free = [None] * 2
        nu_free = [None] * 2
        dr_free = [DV.do(lambda e: e.memset(DR[:, :], 1.0))]
        rcp_free = [None] * 2
        rb_free = [None] * 2
        of_tok = {}
        sn, pn = [0], [0]
        x_tok = {}
        p_zero = []

        def scores(u, h, c, kt):
            kind = u[0]
            pair, par = h // 2, h % 2
            q1, q2, k1, k2 = (view(u, pair, par, n) for n in range(4))
            rows = 128 if kind == "self" else L
            q0 = max(kt * 128, c * 512) if kind == "self" else c * 512
            w = (c + 1) * 512 - q0
            s, i = sn[0] % 2, sn[0] % 3
            sn[0] += 1
            diag = kind == "self" and kt * 128 >= c * 512
            ks = slice(kt * 128, kt * 128 + rows)

            def mms(e):
                e.matmul(ST[s][0:rows, 0:w], k1[:, ks], q1[:, q0:q0 + w], start=True, stop=False)
                last = e.matmul(ST[s][0:rows, 0:w], k2[:, ks], q2[:, q0:q0 + w], start=False, stop=not diag)
                if diag:
                    last = e.matmul(ST[s][:, 0:128], mQK[:, :], idB[:, :], start=False, stop=True)
                return last
            p = PE.do(mms, set_tok[u, pair, par], rows_tok[u, pair, par, c], st_free[s])
            ex = AC.do(lambda e: e.activation(PT[i][0:rows, 0:w], ST[s][0:rows, 0:w], ACT.Exp, scale=D ** -0.5),
                       p, P_free[i], p_zero if kind == "cross" else None)
            st_free[s] = ex
            set_free[(kind, *setkey(u, pair, par))] = [p]
            return (u, h, c, kt, q0, w, i, ex)

        def pv(u, h, c, kt, q0, w, i, ex):
            kind = u[0]
            pair, par = h // 2, h % 2
            g = pair // 2
            v = (uidx[u] * 4 + g) % 2 if kind == "self" else uidx[u] % 2
            vt = kt if kind == "self" else g
            vc = (pair % 2) * 192 + 64 * par
            base, den = 64 * par, 64 * (1 - par)
            first = kt == 0
            last_kt = kt == (4 * c + 3 if kind == "self" else 0)
            o0 = q0 - c * 512
            p = PE.do(lambda e: e.matmul(OB[c][:, o0:o0 + w], VV[v][:, vt, vc:vc + 128], PT[i][:, 0:w],
                                         start=first, stop=last_kt),
                      ex, vv_tok[u, g], o_free[c] if first else None)
            P_free[i] = p
            vv_free[v] = p
            if last_kt:
                nu = NU[pair % 2]
                row = 64 * par + 32 * c
                a = AC.do(lambda e: e.activation(nu[base:base + 64, c * 512:c * 512 + 512],
                                                 OB[c][base:base + 64, :], ACT.Copy), p, nu_free[pair % 2])
                d = AC.do(lambda e: e.activation(DR[row:row + 1, :], OB[c][den:den + 1, :], ACT.Copy), p, dr_free[0])
                o_free[c] = d
                of_tok.setdefault((u, pair), []).extend([a, d])

        oh_free = [None, 0]

        def outproj(u, pair):
            kind, b = u
            key = "0" if kind == "self" else "1"
            box = {}

            nu, rc = NU[pair % 2], RCP[pair % 2]

            def weights():
                box["s"], box["t"] = split([(woview(3)[:, pair, :], 3, raw_tok["wo" + key])], 4)

            def denoms():
                assert len(of_tok[u, pair]) == 8
                bk, ready, i = take()

                def mms(e):
                    for n in range(4):
                        last = e.transpose(bk[:, n * 128:n * 128 + 128], DR[:, n * 128:n * 128 + 128], idF[:, :])
                    return last
                p = PE.do(mms, of_tok[u, pair], ld_cst, ready)
                dr_free[0] = p
                d = DV.do(lambda e: e.reciprocal(
                    rc[:, :, :], bk[:, :].rearrange("p (n r s) -> p n r s", n=4, r=4)[:, :, :, 0]),
                    p, rcp_free[pair % 2])
                free(i, d)
                rcp_free[pair % 2] = []
                box["r"] = []
                for c in range(2):
                    w = rc[:, :, c:4:2].unsqueeze(3).to_broadcast([128, 4, 2, 64])
                    k = DV.do(lambda e, c=c, w=w: e.tensor_copy(
                        RBC[c][:, :].rearrange("p (n h m) -> p n h m", n=4, h=2), w), d, rb_free[c])
                    box["r"].append(k)
                    rcp_free[pair % 2].append(k)
                box["o"] = []

            def normalise(c):
                bk, ready, i = take()
                cs = slice(c * 512, c * 512 + 512)

                def mms(e):
                    for n in range(4):
                        last = e.transpose(bk[:, n * 128:n * 128 + 128], RBC[c][:, n * 128:n * 128 + 128],
                                           idF[:, :])
                    return last
                p = PE.do(mms, box["r"][c], ready)
                rb_free[c] = p
                assert oh_free[1] == 0
                if c == 1:
                    oh_free[1] = 4
                d = DV.do(lambda e: e.tensor_tensor(nu[:, cs], bk[:, :], nu[:, cs], ALU.mult), p, of_tok[u, pair])
                free(i, d)
                a = AC.do(lambda e: e.activation(OH[:, cs], nu[:, cs], ACT.Copy), d, oh_free[0])
                g = PO.do(lambda e: e.tensor_tensor(OL[:, cs], nu[:, cs], OH[:, cs].bitcast(F), ALU.subtract),
                          a, oh_free[0])
                nu_free[pair % 2] = g
                box["o"].append([a, g])

            def piece(j):
                s = box["s"]
                bk, ready, i = take()
                wh, wlo = SLH[s][:, 0:256], SLL[s][:, 0:256]

                def mms(e):
                    for n in range(2):
                        ts = slice((2 * j + n) * 128, (2 * j + n) * 128 + 128)
                        last = mm3(e, bk[:, n * 256:n * 256 + 256],
                                   [(OH[:, ts], wh), (OH[:, ts], wlo), (OL[:, ts], wh)])
                    return last
                p = PE.do(mms, box["t"], box["o"][j // 2], ready)
                sl["free"][s] = p
                left_of[s] -= 1
                oh_free[:] = [p, oh_free[1] - 1]
                xs = X[:, b, 2 * j:2 * j + 2, :].rearrange("p t c -> p (t c)")
                d = DV.do(lambda e: e.tensor_tensor(xs, xs, bk[:, :], ALU.add), p, x_tok[b], x_prev.get((b, j)))
                x_prev[b, j] = d
                free(i, d)

            return [weights, denoms, lambda: normalise(0), lambda: normalise(1)] + [lambda j=j: piece(j) for j in range(4)]

        x_prev = {}
        ln_free = []

        def norm_parts(b, tiles):
            t0, t1 = tiles[0], tiles[-1] + 1
            box = {}

            def stats():
                src = [x_prev[b, t // 2] for t in tiles]
                ss = [DV.do(lambda e, t=t: e.bn_stats(st[:, t, :], X[:, b, t, :]), src, ln_free) for t in tiles]
                aa = [DV.do(lambda e, t=t: e.bn_aggr(mv[:, t, :], st[:, t, :]), ss[n]) for n, t in enumerate(tiles)]
                a = PO.do(lambda e: e.tensor_scalar(rs[:, t0:t1], mv[:, t0:t1, 1], EPS, None, ALU.add), aa)
                box["a"] = PO.do(lambda e: e.tensor_tensor(rs[:, t0:t1], rs[:, t0:t1], half[:, t0:t1], ALU.pow),
                                 a, k_half)

            def rows():
                d = [DV.do(lambda e, t=t: e.tensor_scalar(X[:, b, t, :], X[:, b, t, :], mv[:, t, 0:1],
                                                          rs[:, t:t + 1], ALU.subtract, ALU.mult), box["a"])
                     for t in tiles]
                ln_free[:] = [d[-1]]
                x_tok[b] = box["d"] = d[-1]
                for t in tiles:
                    x_prev[b, t // 2] = d[-1]
                return d[-1]
            return [stats, rows]

        def norm(b, tiles=range(NT)):
            stats, rows = norm_parts(b, tiles)
            stats()
            return rows()

        def norm_pieces(b):
            (s0, r0_), (s1, r1_), (s2, r2_), (s3, r3_) = (norm_parts(b, [2 * k, 2 * k + 1]) for k in range(4))
            return [s0, s1, r0_, s2, r1_, s3, r2_, r3_]

        def transpose_x(b):
            pieces = []
            toks = [[], []]

            def piece(kt, c):
                bk, ready, i = take()

                def mms(e):
                    for n in range(4):
                        last = e.transpose(bk[:, n * 128:n * 128 + 128],
                                           X[:, b, 4 * c + n, kt * 128:kt * 128 + 128], idF[:, :])
                    return last
                p = PE.do(mms, x_tok[b], ld_cst, ready)
                h = XH[:, kt, c * 512:c * 512 + 512]
                l = XL[:, kt, c * 512:c * 512 + 512]
                a = AC.do(lambda e: e.activation(h, bk[:, :], ACT.Copy), p, xh_free[0])
                d = DV.do(lambda e: e.tensor_tensor(l, bk[:, :], h.bitcast(F), ALU.subtract), a, xh_free[0])
                free(i, d)
                toks[c] += [a, d]
                if kt and c:
                    xh_tok[0] = toks
            for c in range(2):
                for kt in range(2):
                    pieces.append(lambda kt=kt, c=c: piece(kt, c))
            return pieces

        ctx_tok = [None]

        def add_bias(b, t):
            x_tok[b] = DV.do(lambda e: e.tensor_tensor(X[:, b, t, :], X[:, b, t, :], boS, ALU.add), ld_x[b], ld_bo)

        def renew_ones():
            k_ones[0] = vv_free[0] = ones(0, raw_read)

        def load_ctx():
            z = PO.do(lambda e: e.memset(SH[1][:, :], 0.0), tmp_free[1])
            cv_ = SH[1][:, 0:NB * 2 * LP].rearrange("p (b k n) -> p b k n", b=NB, k=2)
            for b in range(NB):
                for k in range(2):
                    t = load("ctx", cv_[:, b, k, 0:L], cT[b, k * 128:k * 128 + 128, :], z)
            sf = [t2 for k2_, ts in set_free.items() if k2_[2] == 0 for t2 in ts]
            a = PO.do(lambda e: e.tensor_copy(CH, cv_), t, z, sf)
            d = PO.do(lambda e: e.tensor_tensor(CL, cv_, CH.bitcast(F), ALU.subtract), a, sf)
            tmp_free[1] = [tmp_free[1], d]
            ctx_tok[0] = d
            kx = REG[:, 2048:2048 + 12 * LP].bitcast(F).rearrange("p (b q k n) -> p b q k n", b=3, q=2, k=2)
            w = d
            for par in range(2):
                aug = 64 * (1 - par)
                w = PO.do(lambda e, a=kx[aug:aug + 64, :, par, 1, :]: e.memset(a, 0.0), w, sf)
                w = PO.do(lambda e, a=kx[aug:aug + 2, :, par, 1, :]: e.memset(a, 1.0), w)
            PO.wait(w)
            k_aug["x"] = w

        def spread(slots, fs, a, b):
            for k, f in enumerate(fs):
                slots[a + k * (b - a) // len(fs)].append(f)

        def vgroups(u):
            gs = [vgroup(u, g) for g in range(4)]
            return [gs[0][0], gs[1][0], *gs[0][1], gs[2][0], *gs[1][1], gs[3][0], *gs[2][1], *gs[3][1]]

        def all_of(*lists):
            for fs in lists:
                for f in (fs if isinstance(fs, (list, tuple)) else [fs]):
                    f()

        def set_aug(buf):
            z = (PO.sem, PO.count)
            for par in range(2):
                aug = 64 * (1 - par)
                q2, k2 = setview(1, par, buf), setview(3, par, buf)
                z = PO.do(lambda e, a=q2[aug:aug + 64, :].bitcast(F): e.memset(a, 0.0), z)
                z = PO.do(lambda e, a=k2[aug:aug + 64, :].bitcast(F): e.memset(a, 0.0), z)
                z = PO.do(lambda e, a=k2[aug:aug + 2, :].bitcast(F): e.memset(a, 1.0), z)
            for par in range(2):
                k_aug[par] = z
                set_tok[units[0], buf, par].append(z)
                set_free["self", par, buf] = set_free.get(("self", par, buf), []) + [z]
            PO.wait(z)

        st0, ps, ls = prep(units[0], 0)
        mx, after_mx = max_self(units[0], 0)
        vg0 = vgroup(units[0], 0)
        all_of(st0, vg0[0], ps[0:2], ls[0:1], ps[2:3], ls[1:2], ps[3:4], vg0[1][0:2], ls[2:3], mx[0:4], ls[3:4], vg0[1][2:])
        for i in range(2):
            P_free[i], nu_free[0] = tmp_free[2 + i], [tmp_free[2], tmp_free[3]]
        all_of(mx[4:8], lambda: set_aug(0), after_mx["turn0"], mx[8:], after_mx["put0"], after_mx["least"])
        carried_items = [(13.0, after_mx["turn1"]), (14.0, after_mx["put1"])]

        pend = []

        def drain(n):
            while len(pend) > n:
                pv(*pend.pop(0))

        nprep = prep(units[0], 1)
        nprep[0]()
        set_aug(1)
        k_ones[1] = ones(1, raw_read)
        vv_free[1] = k_ones[1]
        carried = []
        for u in units[:2]:
            b = u[1]
            for h in range(NH):
                pair, par = h // 2, h % 2
                slots = [[] for _ in range(12)]
                prev = (u, pair - 1) if pair else (units[0], NP - 1) if u == units[1] else None
                nxt = (u, h + 1) if h + 1 < NH else (units[1], 0) if u == units[0] else None
                mx, rest = max_self(*nxt) if nxt else max_cross(units[2], 0)
                items = [(where - 12, f) for where, f in carried_items]

                def at(table, names, fs):
                    items.extend((table[k], f) for k, f in zip(names, fs))
                at(EVERY if nxt else LAST, [f"m{k}" for k in range(len(mx))], mx)
                at(EVERY if nxt else LAST, list(rest), rest.values())
                if u == units[0] and h == 12:
                    raw_read.clear()
                    slots[8] += [lambda c=c, kt=kt: fetch_xT(1, 0, c, kt, vv_free[0]) for c in range(2) for kt in range(2)]
                if u == units[0] and h == 13:
                    spread(slots, load_xT(1, 0), 2, 10)
                if u == units[0] and h == 14:
                    slots[0].append(renew_ones)
                if u == units[0] and h == 0:
                    spread(slots, [lambda b=b, t=t: add_bias(b, t) for b in range(NB) for t in range(NT)], 2, 12)
                if par == 0:
                    if prev:
                        weights, denoms, n0, n1, *carried = outproj(*prev)
                        at(EVEN, ["weights", "denoms", "n0", "n1"], [weights, denoms, n0, n1])
                    if pair + 1 == NP and u == units[1]:
                        slots[0].append(load_ctx)
                        slots[0].append(lambda: (load_w("wq1", 0, cq), load_w("wk1", 1, ck), load_w("wv1", 2, cv)))
                        at(LAST, ["x0", "x1", "x2", "x3"], transpose_x(0))
                        nprep = prep(units[2], 0)
                        at(LAST, ["psplit"], nprep[0:1])
                    _, ps, ls = nprep
                    if pair + 1 < NP:
                        at(EVEN, ["p0", "p1", "p2", "p3"], ps)
                        at(EVEN, ["l0", "l1", "l2", "l3"], ls)
                    else:
                        at(LAST, ["p0", "p1", "p2", "p3"], ps)
                        at(LAST, ["l0", "l1", "l2", "l3"], ls)
                    vg = None
                    if pair % 2:
                        if pair + 1 < NP:
                            vg = vgroup(u, pair // 2 + 1)
                        elif u == units[0]:
                            vg = vgroup(units[1], 0)
                    if vg:
                        at(EVEN, ["vsplit"], [vg[0]])
                else:
                    at(ODD, ["o0", "o1", "o2", "o3"], carried)
                    if prev and pair == 0:
                        items += [(LAST["norm"] + 0.25 * k, f) for k, f in enumerate(norm_pieces(0))]
                    if vg:
                        at(ODD, ["v0", "v1", "v2", "v3"], vg[1])
                    elif pair + 1 == NP:
                        at(LAST, ["v"], [lambda fs=vgroups(units[2]): all_of(fs)])
                    nu = (u, pair + 2) if pair + 2 < NP else (units[uidx[u] + 1], 0)
                    if pair + 2 == NP:
                        nu = (units[1], 0) if u == units[0] else None
                    elif pair + 1 == NP:
                        nu = (units[1], 1) if u == units[0] else (units[2], 1)
                    if nu:
                        nprep = prep(*nu)
                        at(ODD, ["psplit"], [nprep[0]])
                carried_items = [p for p in items if p[0] >= 12]
                for where, f in sorted(items, key=lambda p: p[0]):
                    if where < 12:
                        slots[int(where)].append(f)
                n = 0
                for c in range(2):
                    for kt in range(4 * (c + 1)):
                        pend.append(scores(u, h, c, kt))
                        drain(2)
                        for f in slots[n]:
                            f()
                        n += 1

        drain(0)
        p_zero += [DV.do(lambda e, i=i: e.memset(PT[i][64:128, :], 0.0), P_free[i]) for i in range(3)]

        pairs = [(u, p) for u in units[2:] for p in range(NP)]
        NQ = 256
        WH = [REG[:, 1024 * i:1024 * i + 2048] for i in (4, 12, 6, 14)]
        w1h, w1l = (w.rearrange("p (k n) -> p k n", k=2) for w in WH[0:2])
        w2h, w2l = (w.rearrange("p (k n) -> p k n", k=8) for w in WH[2:4])
        HH = [REG[:, 1024 * i:1024 * i + 2048].rearrange("p (k n) -> p k n", k=8) for i in (10, 0)]
        HL = [REG[:, 1024 * i:1024 * i + 2048].rearrange("p (k n) -> p k n", k=8) for i in (8, 2)]
        h_free = [None] * 2
        last_use = {}
        ready_of = {}

        def split_ffn(n, slot, ap, buf):
            src = Wraw[slot]
            t = load(f"W{n}", src[:, :], ap, raw_free[slot])
            fr = [x for k, ts in set_free.items() if k[0] == "cross" and k[2] == buf for x in ts]
            ready_of[n] = []

            def piece(c):
                cs = slice(c * 512, c * 512 + 512)
                a = AC.do(lambda e: e.activation(WH[2 * n][:, cs], src[:, cs], ACT.Copy), t, fr)
                ready_of[n].append(PO.do(lambda e: e.tensor_tensor(WH[2 * n + 1][:, cs], src[:, cs],
                                                                   WH[2 * n][:, cs].bitcast(F), ALU.subtract),
                                         a, t, fr))
            return [lambda c=c: piece(c) for c in range(4)]

        def route(b):
            wl, sel, nsel, cnt = wlS[b], selS[b], nselS[b], cntS[b]
            box = {}

            box["d"], box["c"] = [], []

            def logits(t0):
                for t in range(t0, t0 + 4):
                    tmp = SH[0][:, t % 2 * C:t % 2 * C + C]
                    a = PO.do(lambda e, t=t, tmp=tmp: e.tensor_tensor(tmp, X[:, b, t, :], wrS, ALU.mult),
                              x_tok[b], ld_wr, last_use.get(("t", t % 2)), last_use.get(("r", 1)))
                    box["d"].append(DV.do(lambda e, t=t, tmp=tmp: e.tensor_reduce(wl[:, t:t + 1], tmp, AX.X, ALU.add),
                                          a))
                    last_use["t", t % 2] = box["d"][-1]
                if t0:
                    box["w"] = DV.do(lambda e: e.tensor_scalar(wl[:, :], wl[:, :], brS[:, 0:1], None, ALU.add),
                                     box["d"], ld_sm)

            def repeat(j):
                for n in range(4):
                    t = 4 * j + n
                    wb = SH[1 - j][:, 128 * n:128 * n + 128]
                    box["r"] = DV.do(lambda e, t=t, wb=wb: e.tensor_copy(wb, wl[:, t:t + 1].to_broadcast([128, 128])),
                                     box["w"], last_use.get(("r", j)), last_use.get("e"))

            def count(j):
                bk, ready, i = take()
                ps = PE.do(lambda e: [e.transpose(bk[:, n * 128:n * 128 + 128], SH[1 - j][:, 128 * n:128 * n + 128],
                                                  idF[:, :]) for n in range(4)][-1], box["r"], ready)
                last_use["r", j] = ps
                box[j] = AC.do(lambda e: e.activation(every[j], bk[:, :], ACT.Copy), ps, last_use.get("e"))
                free(i, box[j])

            def above(j, t0):
                for t in range(t0, t0 + 4):
                    k = DV.do(lambda e, t=t: e.tensor_scalar(
                        scr[:, :], every[j], wl[:, t:t + 1], None, ALU.is_ge, ALU.add,
                        accum_out=cnt[:, t, j:j + 1]), box[j], box["c"][-1] if box["c"] else None)
                    box["c"].append(k)
                last_use["e"] = k

            def select():
                a = DV.do(lambda e: e.tensor_tensor(cnt[:, :, 0], cnt[:, :, 0], cnt[:, :, 1], ALU.add), box["c"])
                a = DV.do(lambda e: e.tensor_scalar(sel[:, :], cnt[:, :, 0], TOP - 0.5, None, ALU.is_lt), a)
                n = DV.do(lambda e: e.tensor_scalar(nsel[:, :], sel[:, :], -1.0, 2.0, ALU.mult, ALU.add), a)
                sel_tok[b] = [a, n]
            return [lambda: logits(0), lambda: logits(4), lambda: (repeat(0), repeat(1)),
                    lambda: (count(0), count(1)), lambda: above(0, 0), lambda: above(0, 4), lambda: above(1, 0),
                    lambda: above(1, 4), select]

        ld_wr = load("wr", wrS, wr, rope_last)
        tb2 = load("b2", b2S, b2, rope_last)
        scr, every = cosS[:, 512:1024], [sinS[:, 512:1024], SH[1][:, :]]
        sel_tok = {}

        all_of(nprep[1], nprep[2])
        nprep = prep(*pairs[2])
        nprep[0]()
        left = []
        for n, (u, pair) in enumerate(pairs):
            weights, denoms, n0, n1, *ops = outproj(*pairs[n - 1]) if n else outproj(units[1], NP - 1)
            mx, rest = max_cross(*pairs[n + 1]) if n + 1 < len(pairs) else ([], {})
            ps, ls = nprep[1:] if nprep else ([], [])
            items = [(float(k), lambda k=k: pend.append(scores(u, 2 * pair + k // 2, k % 2, 0))) for k in range(4)]
            items += [(CROSS[f"pv{k}"], lambda k=k: drain(0 if k == 3 else 1)) for k in range(4)]
            fs = {"weights": weights, "denoms": denoms, "n0": n0, "n1": n1, "o0": ops[0], "o1": ops[1]}
            for k, lst in (("m", mx), ("p", ps), ("l", ls)):
                fs.update({f"{k}{m}": f for m, f in enumerate(lst)})
            fs.update(rest)
            if left:
                fs.update(o2=left[0], o3=left[1])
            items += [(CROSS[k], f) for k, f in fs.items()] + [(where - 4, f) for where, f in carried_items]
            carried_items = [p for p in items if p[0] >= 4]
            if n == 10:
                r0 = route(0)
            if n >= 10:
                items += [(CROSS[f"r{k}"], f) for k, f in enumerate(r0[3 * (n - 10):3 * (n - 10) + 3])]
            if n == 14:
                items += [(CROSS[f"t{k}"], f) for k, f in enumerate(transpose_x(0))]
            if n >= 14:
                items += [(CROSS[f"w{k}"], f) for k, f in enumerate(
                    split_ffn(0, 0, W1, 1) if n == 14 else split_ffn(1, 2, W2, 2))]
            if n == 0:
                items.append((CROSS["weights"] + 1e-3, lambda: load_w("wo1", 3, co)))
            if n in (1, 9):
                items += [(CROSS["norm"] + 0.25 * k, f) for k, f in enumerate(norm_pieces(1 if n == 1 else 0))]
            for where, f in sorted(items, key=lambda p: p[0]):
                if where < 4:
                    f()
            left = ops[2:]
            if n == 6:
                all_of(left)
                left = []
                all_of(vgroups(units[3]))
            if n + 3 < len(pairs):
                if n == 5:
                    all_of(transpose_x(1))
                nprep = prep(*pairs[n + 3])
                nprep[0]()
            else:
                nprep = None
        ff_ready = [t for ts in set_free.values() for t in ts]

        def hidden(b, q):
            i2 = (b * 4 + q) % 2
            qs = slice(q * NQ, q * NQ + NQ)
            toks = []

            def tile(m):
                bk, ready, i = take()

                def mms(e):
                    for n in range(2):
                        hs = slice((2 * m + n) * 128, (2 * m + n) * 128 + 128)
                        terms = []
                        for k in range(2):
                            terms += [(w1h[:, k, hs], XH[:, k, qs]), (w1h[:, k, hs], XL[:, k, qs]),
                                      (w1l[:, k, hs], XH[:, k, qs])]
                        last = mm3(e, bk[:, n * 256:n * 256 + 256], terms)
                    return last
                p = PE.do(mms, xh_tok[0], ready_of[0], ready)
                xh_free[0] = p
                j = m % 2
                for n in range(2):
                    g = AC.do(lambda e, n=n, j=j: e.activation(
                        T1[j][:, n * 256:n * 256 + 256], bk[:, n * 256:n * 256 + 256], ACT.Gelu,
                        bias=b1S[:, 2 * m + n:2 * m + n + 1], scale=1.0), p, ld_sm, tmp_free[j])
                free(i, g)
                hh = HH[i2][:, 2 * m:2 * m + 2, :].rearrange("p k n -> p (k n)")
                hl = HL[i2][:, 2 * m:2 * m + 2, :].rearrange("p k n -> p (k n)")
                a = DV.do(lambda e, j=j, hh=hh: e.tensor_copy(hh, T1[j][:, :]), g, h_free[i2], ff_ready)
                on = PO if b or q else DV
                d = on.do(lambda e, j=j, hh=hh, hl=hl: e.tensor_tensor(hl, T1[j][:, :], hh.bitcast(F),
                                                                       ALU.subtract), a, h_free[i2], ff_ready)
                tmp_free[j] = d
                toks.extend([a, d])
            for m in range(4):
                tile(m)
            return toks

        def finish(b, q, toks):
            i2 = (b * 4 + q) % 2
            bk, ready, i = take()

            def mms(e):
                for n in range(2):
                    ts = slice(n * 128, n * 128 + 128)
                    terms = []
                    for k in range(8):
                        terms += [(HH[i2][:, k, ts], w2h[:, k, :]), (HH[i2][:, k, ts], w2l[:, k, :]),
                                  (HL[i2][:, k, ts], w2h[:, k, :])]
                    last = mm3(e, bk[:, n * 256:n * 256 + 256], terms)
                return last
            p = PE.do(mms, toks, ready_of[1], ready)
            h_free[i2] = p
            for n in range(2):
                t = 2 * q + n
                xs = X[:, b, t, :]
                y = PT[n][:, 0:256]
                a = DV.do(lambda e, n=n, y=y: e.tensor_tensor(y, bk[:, n * 256:n * 256 + 256], b2S, ALU.add),
                          p, tb2, P_free[n], last_use.get(("y", n)))
                z = DV.do(lambda e, t=t, xs=xs: e.tensor_scalar(xs, xs, nselS[b][:, t:t + 1], None, ALU.mult),
                          sel_tok[b], x_tok[b])
                d = DV.do(lambda e, t=t, xs=xs, y=y: e.scalar_tensor_tensor(xs, y, selS[b][:, t:t + 1], xs,
                                                                            ALU.mult, ALU.add), a, z)
                last_use["y", n] = d
                x_prev[b, t // 2] = d
            free(i, a)
            d = norm(b, [2 * q, 2 * q + 1])
            outs.append(load("out", out[b, q * 256:q * 256 + 256, :].rearrange("(n p) c -> p n c", p=128),
                             X[:, b, 2 * q:2 * q + 2, :], d))

        outs = []
        quarters = [(b, q) for b in range(NB) for q in range(4)]
        last = outproj(*pairs[-1])
        all_of(left, last[0:2])
        tk = hidden(*quarters[0])
        all_of(last[2:])
        norm(1)
        r1 = route(1)
        before = {1: r1[1:2], 2: r1[3:4], 3: r1[4:5], 4: r1[7:9]}
        behind = {0: r1[0:1], 1: r1[2:3], 3: r1[5:7]}
        for n, bq in enumerate(quarters):
            nx = hidden(*quarters[n + 1]) if n != 3 and n < 7 else None
            if n == 3:
                all_of(transpose_x(1))
            all_of(before.get(n, []))
            finish(*bq, tk)
            all_of(behind.get(n, []))
            tk = hidden(*quarters[4]) if n == 3 else nx
        SP.wait(outs[-1])

        @block.sync
        def _(e):
            SP.run(e)

        @block.scalar
        def _(e):
            AC.run(e)

        @block.vector
        def _(e):
            DV.run(e)

        @block.gpsimd
        def _(e):
            PO.run(e)

        @block.tensor
        def _(e):
            PE.run(e)


def kernel(**inputs):
    import numpy as np
    import concourse.bacc as _bacc
    from concourse import mybir as _mybir
    from concourse.bass_utils import run_bass_kernel_spmd as _run

    g = {k: np.asarray(v) for k, v in inputs.items()}

    def rows(w, k):
        return w.reshape(k, 128, -1).transpose(1, 0, 2).reshape(128, -1)

    inv = (1.0 / np.float32(10000.0) ** (np.arange(0, D, 2, dtype=np.float32) / np.float32(D))).astype(np.float32)
    ang = np.arange(T, dtype=np.float32)[:, None] * inv[None, :]
    sn, cs = np.sin(ang).astype(np.float32), np.cos(ang).astype(np.float32)
    cosT = np.tile(np.repeat(cs.T, 2, axis=0), (2, 1))
    sinT = np.repeat(sn.T, 2, axis=0)
    sinT[0::2] = -sinT[0::2]
    sinT = np.tile(sinT, (2, 1))
    i = np.arange(128)
    feed = {
        "xT": g["x"].transpose(0, 2, 1), "x": g["x"], "cT": g["ctx_1024"].transpose(0, 2, 1),
        "Wq": rows(g["L0_attn_Wq"], 2), "Wk": rows(g["L0_attn_Wk"], 2), "Wv": rows(g["L0_attn_Wv"], 2),
        "Wo": rows(g["L0_attn_Wo"], 8), "bo": np.tile(g["L0_attn_bo"][None], (128, 1)),
        "cq": rows(g["L0_xattn_w_q"], 2), "ck": rows(g["L0_xattn_w_k"], 2), "cv": rows(g["L0_xattn_w_v"], 2),
        "co": rows(g["L0_xattn_w_o"], 8), "wr": np.tile(g["L0_ffn_w_r"].reshape(1, -1), (128, 1)),
        "br": np.tile(g["L0_ffn_b_r"].reshape(1, 1), (128, 1)),
        "W1": rows(g["L0_ffn_W1"], 2), "b1": g["L0_ffn_b1"].reshape(8, 128).T,
        "W2": rows(g["L0_ffn_W2"], 8), "b2": np.tile(g["L0_ffn_b2"][None], (128, 1)),
        "cosT": cosT, "sinT": sinT, "identd": np.eye(128, dtype=np.float32),
        "maskqk": np.where(i[None, :] > i[:, None], np.float32(NEG), np.float32(0)),
    }
    nc = _bacc.Bacc("TRN2", target_bir_lowering=False, num_devices=1)
    arrays, args = {}, []
    for name, a in feed.items():
        a = np.ascontiguousarray(a)
        arrays["in_" + name] = a
        args.append(nc.dram_tensor("in_" + name, a.shape, _mybir.dt.from_np(a.dtype), kind="ExternalInput").ap())
    args.append(nc.dram_tensor("out_0", (NB, T, C), _mybir.dt.float32, kind="ExternalOutput").ap())
    build(nc, *args)
    r = _run(nc, [arrays], core_ids=[0])
    return r.results[0]["out_0"]
```
